# Optimizing a Trainium2 kernel written in Bass

```python
import numpy as np
import jax
import jax.numpy as jnp

def _softmax(x, axis=-1):
    return jax.nn.softmax(x, axis=axis)

def _gelu(x):
    return jax.nn.gelu(x, approximate=True)

def _silu(x):
    return jax.nn.silu(x)

def _sigmoid(x):
    return jax.nn.sigmoid(x)

def _layernorm(x, axis=-1, eps=1e-05):
    m = jnp.mean(x, axis=axis, keepdims=True)
    v = jnp.var(x, axis=axis, keepdims=True)
    return (x - m) / jnp.sqrt(v + eps)

def _scatter_add(tgt, idx, src, axis=0):
    return tgt.at[idx].add(src)

def _segment_sum(src, seg, n):
    return jax.ops.segment_sum(src, seg, n)
kernel_name = 'mk_flamingo_gated_d1_seqx_r8_57c632'

def setup_inputs(seed: int=0):
    np.random.seed(seed)
    _w = jnp.asarray

    def _rec_inputs():
        import jax
        import jax.numpy as jnp
        _rk = jax.random.key(seed)
        x = -0.0003929 + 0.9999 * jax.random.normal(jax.random.fold_in(_rk, 1), (8, 56, 256), jnp.float32)
        _lenS = 56 - jax.random.randint(jax.random.fold_in(_rk, 7), (8,), 0, max(1, 56 // 4) + 1, jnp.int32)
        _lenS2 = 1500 - jax.random.randint(jax.random.fold_in(_rk, 8), (8,), 0, max(1, 1500 // 4) + 1, jnp.int32)
        _ctx_2048P = jax.random.normal(jax.random.fold_in(_rk, 11), (8, 16, 256), jnp.float32)
        _ctx_2048c = jax.random.dirichlet(jax.random.fold_in(_rk, 511), 0.3 * jnp.ones((16,), jnp.float32), (8, 1500))
        _ctx_2048t = jnp.einsum('bsk,bkd->bsd', _ctx_2048c, _ctx_2048P)
        _ctx_2048t = _ctx_2048t * jax.lax.rsqrt(jnp.mean(jnp.square(_ctx_2048t)) + 1e-12) * 0.953939
        ctx_2048 = -0.000514642 + 1.00011 * (_ctx_2048t + 0.3 * jax.random.normal(jax.random.fold_in(_rk, 611), (8, 1500, 256), jnp.float32))
        _g = jax.random.normal(jax.random.fold_in(_rk, 9001), (2, 1), jnp.float32)
        _g = jnp.sign(_g) * jnp.maximum(jnp.abs(_g), 1.0) + (_g == 0) * 1.0
        g_xattn = _g[0]
        g_ffn = _g[1]
        return (x, ctx_2048, g_xattn, g_ffn)
    x, ctx_2048, g_xattn, g_ffn = _rec_inputs()

    def _L0_xattn_setup():
        import jax, jax.numpy as jnp
        import numpy as np
        NUM_HEADS = 16

        def _qdq(x):
            s = jnp.maximum(jnp.max(jnp.abs(x), axis=-1, keepdims=True) / 127.0, 1e-08)
            return jnp.clip(jnp.round(x / s), -127.0, 127.0) * s
        key = jax.random.key(seed)
        ks = jax.random.split(key, 8)
        B, N, M, D = (2, 512, 64, 256)
        w_std = 0.02
        return {'x': jax.random.normal(ks[0], (B, N, D), jnp.float32), 'cond': jax.random.normal(ks[1], (B, M, D), jnp.float32), 'wq': jax.random.normal(ks[2], (D, D), jnp.float32) * w_std, 'bq': jax.random.normal(ks[3], (D,), jnp.float32) * w_std, 'wkv': jax.random.normal(ks[4], (2 * D, D), jnp.float32) * w_std, 'bkv': jax.random.normal(ks[5], (2 * D,), jnp.float32) * w_std, 'wp': jax.random.normal(ks[6], (D, D), jnp.float32) * w_std, 'bp': jax.random.normal(ks[7], (D,), jnp.float32) * w_std}
    _L0_xattn_all = _L0_xattn_setup()
    _L0_xattn_in = {k: v for k, v in _L0_xattn_all.items() if k in ('wq', 'bq', 'wkv', 'bkv', 'wp', 'bp')}
    del _L0_xattn_all

    def _L0_ffn_setup():
        import jax, jax.numpy as jnp
        import numpy as np
        E = 16
        K = 2
        D = 256
        I = 176
        CAP = 128
        VOCAB = 16160
        key = jax.random.key(seed)
        ks = jax.random.split(key, 11)
        B, S = (4, 128)
        sd = 1.0 / np.sqrt(D)
        si = 1.0 / np.sqrt(I)
        return {'x': jax.random.normal(ks[0], (B, S, D), jnp.float32), 'input_ids': jax.random.randint(ks[1], (B, S), 0, VOCAB, dtype=jnp.int64), 'gate_w': jax.random.normal(ks[2], (E, D), jnp.float32) * sd, 'gate_b': jax.random.normal(ks[3], (E,), jnp.float32) * 0.01, 'W1': jax.random.normal(ks[4], (E, I, D), jnp.float32) * sd, 'W3': jax.random.normal(ks[5], (E, I, D), jnp.float32) * sd, 'W2': jax.random.normal(ks[6], (E, D, I), jnp.float32) * si, 'Ws1': jax.random.normal(ks[7], (I, D), jnp.float32) * sd, 'Ws3': jax.random.normal(ks[8], (I, D), jnp.float32) * sd, 'Ws2': jax.random.normal(ks[9], (D, I), jnp.float32) * si}
    _L0_ffn_all = _L0_ffn_setup()
    _L0_ffn_in = {k: v for k, v in _L0_ffn_all.items() if k in ('input_ids', 'gate_w', 'gate_b', 'W1', 'W3', 'W2', 'Ws1', 'Ws3', 'Ws2')}
    del _L0_ffn_all
    return {'x': x, 'ctx_2048': ctx_2048, 'g_xattn': g_xattn, 'g_ffn': g_ffn, 'L0_xattn_wq': _L0_xattn_in['wq'], 'L0_xattn_bq': _L0_xattn_in['bq'], 'L0_xattn_wkv': _L0_xattn_in['wkv'], 'L0_xattn_bkv': _L0_xattn_in['bkv'], 'L0_xattn_wp': _L0_xattn_in['wp'], 'L0_xattn_bp': _L0_xattn_in['bp'], 'L0_ffn_input_ids': _L0_ffn_in['input_ids'], 'L0_ffn_gate_w': _L0_ffn_in['gate_w'], 'L0_ffn_gate_b': _L0_ffn_in['gate_b'], 'L0_ffn_W1': _L0_ffn_in['W1'], 'L0_ffn_W3': _L0_ffn_in['W3'], 'L0_ffn_W2': _L0_ffn_in['W2'], 'L0_ffn_Ws1': _L0_ffn_in['Ws1'], 'L0_ffn_Ws3': _L0_ffn_in['Ws3'], 'L0_ffn_Ws2': _L0_ffn_in['Ws2']}

def reference(x, ctx_2048, g_xattn, g_ffn, L0_xattn_wq, L0_xattn_bq, L0_xattn_wkv, L0_xattn_bkv, L0_xattn_wp, L0_xattn_bp, L0_ffn_input_ids, L0_ffn_gate_w, L0_ffn_gate_b, L0_ffn_W1, L0_ffn_W3, L0_ffn_W2, L0_ffn_Ws1, L0_ffn_Ws3, L0_ffn_Ws2):
    import jax
    import jax.numpy as jnp

    def _L0_xattn_ref(x, cond, wq, bq, wkv, bkv, wp, bp):
        import jax, jax.numpy as jnp
        import numpy as np
        NUM_HEADS = 16

        def _qdq(x):
            s = jnp.maximum(jnp.max(jnp.abs(x), axis=-1, keepdims=True) / 127.0, 1e-08)
            return jnp.clip(jnp.round(x / s), -127.0, 127.0) * s
        B, N, C = x.shape
        M = cond.shape[1]
        H = NUM_HEADS
        Dh = C // H
        q = _qdq(x) @ _qdq(wq).T + bq
        kv = cond @ wkv.T + bkv
        k, v = jnp.split(kv, 2, axis=-1)
        q = q.reshape(B, N, H, Dh)
        k = k.reshape(B, M, H, Dh)
        v = v.reshape(B, M, H, Dh)
        scale = 1.0 / np.sqrt(Dh)
        attn = jax.nn.softmax(jnp.einsum('bnhd,bmhd->bhnm', q, k) * scale, axis=-1)
        o = jnp.einsum('bhnm,bmhd->bnhd', attn, v).reshape(B, N, C)
        out = _qdq(o) @ _qdq(wp).T + bp
        return out

    def _L0_ffn_ref(x, input_ids, gate_w, gate_b, W1, W3, W2, Ws1, Ws3, Ws2):
        import jax, jax.numpy as jnp
        import numpy as np
        E = 16
        K = 2
        D = 256
        I = 176
        CAP = 128
        VOCAB = 16160
        shape = x.shape
        xt = x.reshape(-1, D)
        T = xt.shape[0]
        logits = xt.astype(jnp.float32) @ gate_w.astype(jnp.float32).T
        scores = jnp.sqrt(jax.nn.softplus(logits))
        _, idx = jax.lax.top_k(scores + gate_b, K)
        w = jnp.take_along_axis(scores, idx, axis=1)
        w = w / jnp.sum(w, axis=1, keepdims=True)
        e = idx.reshape(-1)
        onehot = jax.nn.one_hot(e, E, dtype=jnp.int32)
        pos = jnp.sum(onehot * (jnp.cumsum(onehot, axis=0) - 1), axis=1)
        valid = pos < CAP
        posc = jnp.where(valid, pos, 0)
        x_pairs = jnp.repeat(xt, K, axis=0)
        x_pairs = jnp.where(valid[:, None], x_pairs, 0.0)
        buf = jnp.zeros((E, CAP, D), xt.dtype).at[e, posc].add(x_pairs)
        g = jnp.einsum('ecd,eid->eci', buf, W1).astype(jnp.float32)
        u = jnp.einsum('ecd,eid->eci', buf, W3).astype(jnp.float32)
        h = (jax.nn.silu(g) * u).astype(xt.dtype)
        out = jnp.einsum('eci,edi->ecd', h, W2)
        y_pairs = out[e, posc] * (w.reshape(-1) * valid)[:, None]
        y = y_pairs.reshape(T, K, D).sum(axis=1)
        gs = jax.nn.silu((xt @ Ws1.T).astype(jnp.float32))
        us = (xt @ Ws3.T).astype(jnp.float32)
        shared = (gs * us).astype(xt.dtype) @ Ws2.T
        return (y + shared).astype(x.dtype).reshape(shape)
    x = x + jnp.tanh(g_xattn[0]) * _L0_xattn_ref(_layernorm(x, axis=-1), ctx_2048, L0_xattn_wq, L0_xattn_bq, L0_xattn_wkv, L0_xattn_bkv, L0_xattn_wp, L0_xattn_bp)
    x = x + jnp.tanh(g_ffn[0]) * _L0_ffn_ref(_layernorm(x, axis=-1), L0_ffn_input_ids, L0_ffn_gate_w, L0_ffn_gate_b, L0_ffn_W1, L0_ffn_W3, L0_ffn_W2, L0_ffn_Ws1, L0_ffn_Ws3, L0_ffn_Ws2)
    return x

_drawn_inputs = setup_inputs


def setup_inputs(seed=0):
    import zlib

    import numpy as np

    out = dict(_drawn_inputs(seed))
    spreads = {}
    factors = {'L0_xattn_wq': 6.479, 'L0_xattn_bq': 179.852, 'L0_xattn_bkv': 5.203}
    for name, (base, spread) in spreads.items():
        noise = np.random.default_rng([zlib.crc32(name.encode()), seed]).standard_normal(out[name].shape)
        drawn = base * np.exp(spread * noise) if base else spread * noise
        out[name] = jnp.asarray(drawn.astype(out[name].dtype))
    for name, factor in factors.items():
        out[name] = (out[name] * factor).astype(out[name].dtype)
    return out
```

```python
import concourse.bass as bass
from concourse import mybir
from contextlib import ExitStack

F32 = mybir.dt.float32
F16 = mybir.dt.float16
ALU = mybir.AluOpType
ACT = mybir.ActivationFunctionType
AX = mybir.AxisListType

B, S, D = 8, 56, 256
M = 1500
H, DH = 16, 16
E, I = 16, 176
CAP = 128
T = B * S
TP, TT = 112, 4
NH = D // 128
KP, KT = 125, 12
CH = 3
CW = M // CH
G = 4
NPAIR = H // 2
QW = G * 2 * 4 * S
IH = I // 2
WS = 64.0
FS = 16.0
SCORE = DH ** -0.5 / WS
MAGIC = 1.5 * 2.0 ** 23
EPS = 1e-5
NCONST = 16
NSMALL = 8 * 16
SPLIT = ((0, 0), (0, 1), (1, 0))


class Steps:

    def __init__(self, eng, sem, base=0):
        self.eng, self.sem, self.base, self.n = eng, sem, base, 0

    def did(self, ins):
        ins.then_inc(self.sem, 1)
        self.n += 1

    def settle(self):
        self.eng.wait_ge(self.sem, self.base + self.n)


def program(nc, x, ctx, g_xattn, g_ffn, wq, bq, wkv, bkv, wp, bp, gate_w, gate_b, W1, W3, W2, Ws1, Ws3, Ws2, out):
    stack = ExitStack()
    with stack:
        def sb(name, shape, dt=F32):
            return stack.enter_context(nc.sbuf_tensor(name, shape, dt))

        def sem(name):
            return stack.enter_context(nc.semaphore(name))

        ident = sb("ident", [128, 128])
        ident16 = sb("ident16", [128, 128], F16)
        ones = sb("ones", [128, 128])
        ones16 = sb("ones16", [TP, TP], F16)
        before16 = sb("before16", [TP, TP], F16)
        hm2 = sb("hm2", [128, 2, 4])
        hmask = sb("hmask", [128, 4])
        par = sb("par", [128, 2])
        rank = sb("rank", [TP, TT, E])
        x_in = sb("x_in", [TP, TT, D])
        wq_in = sb("wq_in", [128, NH, D])
        wp_in = sb("wp_in", [128, NH, D])
        wkv_in = sb("wkv_in", [128, 2 * NH, D])
        gate_in = sb("gate_in", [E, D])
        bq_c = sb("bq_c", [128, NH])
        bk_c = sb("bk_c", [128, NH])
        bv_r = sb("bv_r", [TP, D])
        bp_r = sb("bp_r", [TP, D])
        gb_r = sb("gb_r", [TP, E])
        gx = sb("gx", [TP, 2])
        tg = sb("tg", [TP, 2])
        tgf = sb("tgf", [TP, 1])
        st = sb("st", [TP, TT, 6])
        mv = sb("mv", [TP, TT, 2])
        var = sb("var", [TP, TT])
        mhalf = sb("mhalf", [TP, TT])
        rstd = sb("rstd", [TP, TT])
        am = sb("am", [128, TT])
        sx = sb("sx", [TP, TT])
        swq = sb("swq", [128, NH])
        swp = sb("swp", [128, NH])
        so = sb("so", [TP, TT])
        xn = sb("xn", [TP, TT, D])
        xq16 = sb("xq16", [TP, TT, D], F16)
        wq16 = sb("wq16", [128, NH, D], F16)
        wp16 = sb("wp16", [128, NH, D], F16)
        wqT = sb("wqT", [128, NH, D], F16)
        wpT = sb("wpT", [128, NH, D], F16)
        xqT = sb("xqT", [128, NH, T], F16)
        diag = sb("diag", [128, TT, 128])
        sx_row = sb("sx_row", [128, T])
        sp_row = sb("sp_row", [TP, D])
        qT = sb("qT", [128, NH, T])
        q16 = sb("q16", [128, 2, G, T], F16)
        QS = sb("QS", [128, B * QW], F16)
        QC = sb("QC", [128, QW], F16)
        wkvT = sb("wkvT", [128, 2, NH, 2 * D], F16)
        c_in = sb("c_in", [KP, KT, D])
        cT = sb("cT", [128, 2, NH, M], F16)
        KS = sb("KS", [128, G, M], F16)
        V = sb("V", [KP, KT, D])
        P = sb("P", [TP, 2, M])
        PT_all = sb("PT_all", [128, NPAIR, KT * TP])
        PT = PT_all[0:KP]
        qd = PT_all[:, 0:2, 0:2 * T].rearrange("p a (b t) -> p a b t", b=2)
        hn = PT_all[0:TP, 3, 0:TT * I].rearrange("p (t i) -> p t i", t=TT)
        th = PT_all[0:TP, 4, 0:2 * I].rearrange("p (t i) -> p t i", t=2)
        hg = PT_all[0:TP, 5, 0:2 * I].rearrange("p (t i) -> p t i", t=2)
        mx = sb("mx", [TP, NPAIR])
        nmx = sb("nmx", [TP, NPAIR])
        den = sb("den", [TP, NPAIR])
        den_all = sb("den_all", [TP, B * NPAIR])
        oe = sb("oe", [128, 2, S])
        OT = sb("OT", [128, 2, T])
        dT = sb("dT", [NPAIR, B * TP])
        rd = sb("rd", [TP, TT, H])
        x1 = sb("x1", [TP, TT, D])
        xT = qT
        at = [0]

        def over_queries(rows, *shape):
            n = 1
            for k in shape:
                n *= k
            at[0] += n
            assert at[0] <= B * QW
            names = "abc"[:len(shape)]
            return QS[0:rows, at[0] - n:at[0]].rearrange(
                f"p ({' '.join(names)}) -> p {' '.join(names)}", **dict(zip(names, shape)))

        xT16 = over_queries(128, 2, NH, T)
        gateT = sb("gateT", [128, NH, E])
        r = [sb(f"r{i}", [TP, TT, E]) for i in range(8)]
        rs = [sb(f"rs{i}", [TP, TT]) for i in range(5)]
        sel16 = sb("sel16", [TP, TT, E], F16)
        WT = sb("WT", [TP, (E + 1) * TT])
        wcur = sb("wcur", [TP, 2, TT])
        zero16 = sb("zero16", [TP, 512], F16)
        w13_in = [sb(f"w13_in{i}", [IH, 4, D]) for i in range(2)]
        w2_in = [sb(f"w2_in{i}", [128, NH, I]) for i in range(2)]
        w13T = [over_queries(128, 2, NH, 2 * I) for i in range(2)]
        w2T = [over_queries(IH, 2, 2 * D) for i in range(2)]
        hT = over_queries(IH, 2, 2, 2 * 2 * TP)
        y_out = xn

        PS = stack.enter_context(nc.psum_tensor("PS", [128, 8, 512], F32))

        def bank16(b):
            return PS[:, b, :].bitcast(F16)

        names = """consts var_ready rstd_ready sp_ready x_loaded wq_loaded wp_loaded wkv_loaded small_loaded xq_ready wqq_ready wpq_ready
            sx_diag sp_diag pe_pre act_pre dve_pre qs_ready dve_step
            t_ready th_done tl_done k_ready kh_done kl_done qc_done sc_ready max_done exp_done tr_ready
            pt_act pt_dve v_ready v_act v_dve pv_ready o_done den_saved
            pe_post act_post dve_post
            w_read wt_ready wh_done wl_done gu_ready tanh_done h_done ht_ready hh_done hl_done y_ready
            y_final stored""".split()
        s = {n: sem(n) for n in names}
        ctx_in = [sem(f"ctx_in{c}") for c in range(CH)]
        w_in = [sem(f"w_in{i}") for i in range(2)]

        ctx_v = ctx.rearrange("b (p t) d -> b p t d", t=KT)
        w13_v = [w.rearrange("e (r p) d -> e p r d", p=IH) for w in (W1, W3)]
        w2_v = W2.rearrange("e (r p) i -> e p r i", p=128)
        block = stack.enter_context(nc.Block())

        @block.sync
        def _(sp):
            sp.dma_start(x_in[:], x.rearrange("b s d -> (b s) d").rearrange("(t p) d -> p t d", p=TP)).then_inc(s["x_loaded"], 16)
            sp.dma_start(wq_in[:], wq.rearrange("(r p) d -> p r d", p=128)).then_inc(s["wq_loaded"], 16)
            sp.dma_start(wkv_in[:], wkv.rearrange("(r p) d -> p r d", p=128)).then_inc(s["wkv_loaded"], 16)
            for c in range(CH):
                sp.dma_start(c_in[:, 4 * c:4 * c + 4, :], ctx_v[0, :, 4 * c:4 * c + 4, :]).then_inc(ctx_in[c], 16)
            sp.dma_start(wp_in[:], wp.rearrange("(r p) d -> p r d", p=128)).then_inc(s["wp_loaded"], 16)
            with sp.Fori(1, B) as b:
                for c in range(CH):
                    sp.wait_ge(s["t_ready"], b * 6 + (2 * c + 2 - 6))
                    sp.dma_start(c_in[:, 4 * c:4 * c + 4, :], ctx_v[b, :, 4 * c:4 * c + 4, :]).then_inc(ctx_in[c], 16)

            def load(e, q, srcs):
                for k in range(2):
                    sp.dma_start(w13_in[q][:, 2 * k:2 * k + 2, :], srcs[k]).then_inc(w_in[q], 16)
                sp.dma_start(w2_in[q][:], srcs[2]).then_inc(w_in[q], 16)

            for e in range(2):
                load(e, e, (w13_v[0][e], w13_v[1][e], w2_v[e]))
            with sp.Fori(1, E // 2) as it:
                for q in range(2):
                    sp.wait_ge(s["wt_ready"], it * 2 + (q - 1))
                    load(None, q, (w13_v[0][it * 2 + q], w13_v[1][it * 2 + q], w2_v[it * 2 + q]))
            sp.wait_ge(s["wt_ready"], E - 1)
            load(E, 0, (Ws1.rearrange("(r p) d -> p r d", p=IH), Ws3.rearrange("(r p) d -> p r d", p=IH),
                        Ws2.rearrange("(r p) i -> p r i", p=128)))
            sp.wait_ge(s["y_final"], 1)
            sp.dma_start(out.rearrange("b s d -> (b s) d").rearrange("(t p) d -> p t d", p=TP), y_out[:]).then_inc(s["stored"], 16)
            sp.wait_ge(s["stored"], 16)

        @block.gpsimd
        def _(gp):
            c = Steps(gp, s["consts"])
            for t, v in ((ident, 0.0), (ident16, 0.0), (ones, 1.0), (ones16, 1.0), (before16, 1.0), (hm2, 1.0),
                         (zero16, 0.0), (mhalf, -0.5)):
                c.did(gp.memset(t[:], v))
            c.did(gp.iota(rank[:], [[0, TT], [-1, E]], base=E, channel_multiplier=0, allow_small_or_imprecise_dtypes=True))
            c.did(gp.memset(WT[:, E * TT:], 0.5 / FS))
            c.settle()
            for t in (ident, ident16):
                c.did(gp.affine_select(out=t[:], in_=t[:], compare_op=ALU.not_equal, fill=1.0, base=0,
                                       pattern=[[-1, 128]], channel_multiplier=1))
            c.did(gp.affine_select(out=before16[:], in_=before16[:], compare_op=ALU.is_ge, fill=0.0, base=-1,
                                   pattern=[[1, TP]], channel_multiplier=-1))
            c.did(gp.affine_select(out=hm2[:], in_=hm2[:], compare_op=ALU.is_ge, fill=0.0, base=0,
                                   pattern=[[-64, 2], [-16, 4]], channel_multiplier=1))
            c.settle()
            c.did(gp.affine_select(out=hm2[:], in_=hm2[:], compare_op=ALU.is_ge, fill=0.0, base=DH - 1,
                                   pattern=[[64, 2], [16, 4]], channel_multiplier=-1))
            c.settle()
            c.did(gp.tensor_tensor(hmask[:], hm2[:, 0, :], hm2[:, 1, :], ALU.add))
            c.settle()
            c.did(gp.tensor_tensor(par[:], hmask[:, 0:2], hmask[:, 2:4], ALU.add))
            gp.wait_ge(s["var_ready"], 1)
            gp.tensor_tensor(rstd[:], var[:], mhalf[:], ALU.pow).then_inc(s["rstd_ready"], 1)
            gp.wait_ge(s["qs_ready"], 1)
            with gp.Fori(0, B) as b:
                gp.wait_ge(s["sc_ready"], b * NPAIR)
                gp.tensor_copy(QC[:], QS[:, bass.ds(b * QW, QW)]).then_inc(s["qc_done"], 1)
                gp.wait_ge(s["exp_done"], b * NPAIR + NPAIR)
                gp.tensor_copy(den_all[:, bass.ds(b * NPAIR, NPAIR)], den[:]).then_inc(s["den_saved"], 1)
            gp.wait_ge(s["var_ready"], 2)
            gp.tensor_tensor(rstd[:], var[:], mhalf[:], ALU.pow).then_inc(s["rstd_ready"], 1)


        @block.scalar
        def _(act):
            for t, src in ((bq_c, bq.rearrange("(r p) -> p r", p=128)), (bk_c, bkv[0:D].rearrange("(r p) -> p r", p=128)),
                           (bv_r, bkv[D:2 * D].partition_broadcast(TP)), (bp_r, bp.partition_broadcast(TP)),
                           (gb_r, gate_b.partition_broadcast(TP))):
                act.dma_start(t[:], src, allow_slow_non_contiguous=True).then_inc(s["small_loaded"], 16)
            act.dma_start(gate_in[:], gate_w).then_inc(s["small_loaded"], 16)
            for k, g in enumerate((g_xattn, g_ffn)):
                act.dma_start(gx[:, k:k + 1], g.partition_broadcast(TP)).then_inc(s["small_loaded"], 16)
            act.wait_ge(s["small_loaded"], NSMALL)
            ap = Steps(act, s["act_pre"])
            ap.did(act.activation(tg[:], gx[:], ACT.Tanh))
            ap.did(act.activation(bk_c[:], bk_c[:], ACT.Copy, scale=WS))
            act.wait_ge(s["pe_pre"], 1)
            ap.did(act.activation(wkvT[:, 0], PS[:, 0:2, :], ACT.Copy, scale=WS))
            act.wait_ge(s["pe_pre"], 2)
            ap.did(act.activation(xqT[:], bank16(2)[:, 0:NH * T].rearrange("p (h t) -> p h t", h=NH), ACT.Copy))
            act.wait_ge(s["pe_pre"], 3)
            ap.did(act.activation(wqT[:], bank16(3)[:, 0:NH * D].rearrange("p (h t) -> p h t", h=NH), ACT.Copy))
            act.wait_ge(s["pe_pre"], 4)
            ap.did(act.activation(sx_row[:], PS[:, 5, 0:T], ACT.Copy))
            act.wait_ge(s["pe_pre"], 6)
            ap.did(act.activation(wpT[:], bank16(4)[:, 0:NH * D].rearrange("p (h t) -> p h t", h=NH), ACT.Copy))
            act.wait_ge(s["pe_pre"], 7)
            ap.did(act.activation(sp_row[:], PS[0:TP, 3, 0:D], ACT.Copy))
            act.wait_ge(s["pe_pre"], 8)
            ap.did(act.activation(gateT[:], PS[:, 2, 0:NH * E].rearrange("p (h e) -> p h e", h=NH), ACT.Copy))
            act.wait_ge(s["act_pre"], 2)

            with act.Fori(0, B) as b:
                act.wait_ge(s["v_ready"], b * 6)
                for u in range(6):
                    c, hf = divmod(u, 2)
                    act.wait_ge(s["t_ready"], b * 6 + u + 1)
                    act.activation(cT[:, 0, hf, c * CW:(c + 1) * CW], PS[:, u, 0:CW], ACT.Copy).then_inc(s["th_done"], 1)
                act.wait_ge(s["sc_ready"], b * NPAIR)
                for u in range(6):
                    c, oh = divmod(u, 2)
                    act.wait_ge(s["k_ready"], b * 6 + u + 1)
                    for k in range(2):
                        rows = slice(64 * k, 64 * k + 64)
                        act.activation(KS[rows, 2 * oh + k, c * CW:(c + 1) * CW], PS[rows, u, 0:CW], ACT.Identity,
                                       bias=bk_c[rows, oh:oh + 1]).then_inc(s["kh_done"], 1)

                def v_evac(v):
                    act.wait_ge(s["v_ready"], b * 6 + v + 1)
                    act.activation(V[:, 2 * v:2 * v + 2, :].rearrange("p t d -> p (t d)"), PS[0:KP, 6, :],
                                   ACT.Copy).then_inc(s["v_act"], 1)

                def exp(i):
                    act.wait_ge(s["max_done"], b * NPAIR + i + 1)
                    act.wait_ge(s["tr_ready"], b * NPAIR + max(i - 1, 0))
                    act.activation(P[:, i % 2, :].rearrange("p (c k) -> p c k", c=CH),
                                   PS[0:TP, 3 * (i % 2):3 * (i % 2) + 3, 0:CW], ACT.Exp, bias=nmx[:, i:i + 1],
                                   scale=SCORE, accum_out=den[:, i:i + 1]).then_inc(s["exp_done"], 1)

                def pt_evac(i):
                    act.wait_ge(s["tr_ready"], b * NPAIR + i + 1)
                    act.activation(PT[:, i, :].rearrange("p (c k) -> p c k", c=CH),
                                   PS[0:KP, 0:3, 0:4 * TP], ACT.Copy).then_inc(s["pt_act"], 1)

                act.wait_ge(s["pv_ready"], b * 2)
                act.wait_ge(s["den_saved"], b)
                v_evac(0)
                exp(0)
                v_evac(2)
                exp(1)
                pt_evac(0)
                exp(2)
                v_evac(4)
                exp(3)
                pt_evac(2)
                exp(4)
                exp(5)
                pt_evac(4)
                exp(6)
                exp(7)
                pt_evac(6)

            act.wait_ge(s["pe_post"], 1)
            dT_w = dT[:].rearrange("p (a b n) -> p b a n", a=2, b=B)
            for k in range(2):
                last = act.activation(dT_w[:, 4 * k:4 * k + 4], PS[0:NPAIR, k, 0:4 * TP].rearrange("p (b a n) -> p b a n", b=4, a=2), ACT.Copy)
            last.then_inc(s["act_post"], 1)
            act.wait_ge(s["pe_post"], 4)
            act.activation(xqT[:], bank16(5)[:, 0:NH * T].rearrange("p (h t) -> p h t", h=NH), ACT.Copy).then_inc(s["act_post"], 1)
            act.wait_ge(s["pe_post"], 6)
            act.activation(xT16[:, 0], PS[:, 0:2, 0:T], ACT.Copy).then_inc(s["act_post"], 1)
            act.activation(xT[:], PS[:, 0:2, 0:T], ACT.Copy).then_inc(s["act_post"], 1)
            act.wait_ge(s["dve_post"], 6)
            act.activation(r[1][:], r[2][:], ACT.Exp).then_inc(s["act_post"], 1)
            act.wait_ge(s["sp_ready"], 1)
            act.activation(r[4][:], r[5][:], ACT.Sqrt).then_inc(s["act_post"], 1)

            def weights_hi(q, n):
                act.wait_ge(s["wt_ready"], n)
                act.activation(w13T[q][:, 0], PS[:, 4:6, 0:2 * I], ACT.Copy, scale=FS)
                act.activation(w2T[q][:, 0], PS[0:IH, 6, :], ACT.Copy, scale=FS).then_inc(s["wh_done"], 1)

            def expert(e, q, prepare):
                def tanh(t):
                    act.wait_ge(s["gu_ready"], e * TT + t + 1)
                    act.wait_ge(s["h_done"], e * TT + max(t - 1, 0))
                    act.activation(th[:, t % 2, :], PS[0:TP, 2 + t % 2, 0:I], ACT.Tanh, scale=0.5 / FS).then_inc(s["tanh_done"], 1)

                def h_hi(p):
                    act.wait_ge(s["ht_ready"], e * 2 + p + 1)
                    act.wait_ge(s["y_ready"], e * 2)
                    act.activation(hT[:, 0, p, :], PS[0:IH, 7, 0:4 * TP], ACT.Copy).then_inc(s["hh_done"], 1)

                tanh(0)
                tanh(1)
                tanh(2)
                h_hi(0)
                tanh(3)
                if prepare:
                    weights_hi(1 - q, e + 2)
                h_hi(1)

            weights_hi(0, 1)
            with act.Fori(0, E // 2) as it:
                for q in range(2):
                    expert(it * 2 + q, q, True)
            expert(E, 0, False)

        @block.vector
        def _(dve):
            d = Steps(dve, s["dve_step"])

            def quantise(src, n, am_, s_, out16):
                d.settle()
                d.did(dve.tensor_reduce(am_[:, 0:n], src[:], AX.X, ALU.max, apply_absolute_value=True))
                d.settle()
                d.did(dve.tensor_scalar(s_[:], am_[:, 0:n], 1.0 / 127, 1e-8, ALU.mult, ALU.max))
                d.settle()
                d.did(dve.reciprocal(am_[:, 0:n], s_[:]))
                d.settle()
                for k in range(n):
                    d.did(dve.tensor_scalar(src[:, k, :], src[:, k, :], am_[:, k:k + 1], 127.0, ALU.mult, ALU.min))
                d.settle()
                d.did(dve.tensor_scalar(src[:], src[:], -127.0, MAGIC, ALU.max, ALU.add))
                d.settle()
                return dve.tensor_scalar(out16[:], src[:], MAGIC, None, ALU.subtract)

            def layernorm(src, dst, nth):
                d.settle()
                for t in range(TT):
                    d.did(dve.bn_stats(st[:, t, :], src[:, t, :]))
                d.settle()
                for t in range(TT):
                    d.did(dve.bn_aggr(mv[:, t, :], st[:, t, :]))
                d.settle()
                dve.tensor_scalar(var[:], mv[:, :, 1], EPS, None, ALU.add).then_inc(s["var_ready"], 1)
                dve.wait_ge(s["rstd_ready"], nth)
                for t in range(TT):
                    d.did(dve.tensor_scalar(dst[:, t, :], src[:, t, :], mv[:, t, 0:1], rstd[:, t:t + 1], ALU.subtract, ALU.mult))

            dve.wait_ge(s["x_loaded"], 16)
            layernorm(x_in, xn, 1)
            quantise(xn, TT, am[0:TP], sx, xq16).then_inc(s["xq_ready"], 1)
            dve.wait_ge(s["consts"], NCONST)
            for t in range(TT):
                last = dve.tensor_scalar(diag[0:TP, t, 0:TP], ident[0:TP, 0:TP], sx[:, t:t + 1], None, ALU.mult)
            last.then_inc(s["sx_diag"], 1)
            dve.wait_ge(s["wq_loaded"], 16)
            quantise(wq_in, NH, am, swq, wq16).then_inc(s["wqq_ready"], 1)
            dve.wait_ge(s["act_pre"], 3)
            dve.scalar_tensor_tensor(wkvT[:, 1], PS[:, 0:2, :], WS, wkvT[:, 0], ALU.mult, ALU.subtract).then_inc(s["dve_pre"], 1)
            dve.wait_ge(s["small_loaded"], NSMALL)
            dve.wait_ge(s["act_pre"], 6)
            dve.wait_ge(s["pe_pre"], 5)
            for oh in range(NH):
                d.did(dve.scalar_tensor_tensor(qT[:, oh, :], PS[:, 6 + oh, 0:T], swq[:, oh:oh + 1], sx_row[:], ALU.mult, ALU.mult))
            d.settle()
            for g in range(G):
                own = slice(64 * (g % 2), 64 * (g % 2) + 64)
                for k in range(2):
                    d.did(dve.tensor_scalar(qd[64 * k:64 * k + 64, g // 2, g % 2, :], qT[own, g // 2, :], bq_c[own, g // 2:g // 2 + 1], None, ALU.add))
            d.settle()
            q4 = q16[:].rearrange("p k (a b) t -> p k a b t", a=2)
            d.did(dve.tensor_copy(q4[:, 0], qd[:]))
            d.settle()
            d.did(dve.tensor_tensor(q4[:, 1], qd[:], q4[:, 0], ALU.subtract))
            d.settle()
            qs_v = QS[:].rearrange("p (b g k h n) -> p b g k h n", b=B, g=G, k=2, h=4)
            for g in range(G):
                for k in range(2):
                    for h in range(4):
                        last = dve.tensor_scalar(qs_v[:, :, g, k, h, :], q16[:, k, g, :].rearrange("p (b n) -> p b n", b=B),
                                                 hmask[:, h:h + 1], None, ALU.mult)
            last.then_inc(s["qs_ready"], 1)
            dve.wait_ge(s["wp_loaded"], 16)
            quantise(wp_in, NH, am, swp, wp16).then_inc(s["wpq_ready"], 1)
            dve.wait_ge(s["pe_pre"], 4)
            for k in range(NH):
                last = dve.tensor_scalar(diag[:, k, :], ident[:], swp[:, k:k + 1], None, ALU.mult)
            last.then_inc(s["sp_diag"], 1)
            pre_steps = d.n

            with dve.Fori(0, B) as b:
                for u in range(6):
                    c, hf = divmod(u, 2)
                    dve.wait_ge(s["th_done"], b * 6 + u + 1)
                    dve.tensor_tensor(cT[:, 1, hf, c * CW:(c + 1) * CW], PS[:, u, 0:CW],
                                      cT[:, 0, hf, c * CW:(c + 1) * CW], ALU.subtract).then_inc(s["tl_done"], 1)
                for u in range(6):
                    c, oh = divmod(u, 2)
                    dve.wait_ge(s["kh_done"], b * 12 + 2 * u + 2)
                    for k in range(2):
                        own, other = slice(64 * k, 64 * k + 64), slice(64 - 64 * k, 128 - 64 * k)
                        cols = slice(c * CW, (c + 1) * CW)
                        last = dve.scalar_tensor_tensor(KS[other, 2 * oh + k, cols], PS[own, u, 0:CW], bk_c[own, oh:oh + 1],
                                                        KS[own, 2 * oh + k, cols], ALU.add, ALU.subtract)
                    last.then_inc(s["kl_done"], 1)
                step = Steps(dve, s["dve_step"], b * (NPAIR + 1) + pre_steps)

                def row_max(i):
                    dve.wait_ge(s["sc_ready"], b * NPAIR + i + 1)
                    step.did(dve.tensor_reduce(mx[:, i:i + 1], PS[0:TP, 3 * (i % 2):3 * (i % 2) + 3, 0:CW], AX.XY, ALU.max))
                    step.settle()
                    dve.tensor_scalar(nmx[:, i:i + 1], mx[:, i:i + 1], -SCORE, None, ALU.mult).then_inc(s["max_done"], 1)

                def v_evac(v):
                    dve.wait_ge(s["v_ready"], b * 6 + v + 1)
                    dve.tensor_copy(V[:, 2 * v:2 * v + 2, :].rearrange("p t d -> p (t d)"), PS[0:KP, 7, :]).then_inc(s["v_dve"], 1)

                def pt_evac(i):
                    dve.wait_ge(s["tr_ready"], b * NPAIR + i + 1)
                    dve.tensor_copy(PT[:, i, :].rearrange("p (c k) -> p c k", c=CH), PS[0:KP, 3:6, 0:4 * TP]).then_inc(s["pt_dve"], 1)

                dve.wait_ge(s["pv_ready"], b * 2)
                dve.wait_ge(s["exp_done"], b * NPAIR)
                row_max(0)
                v_evac(1)
                row_max(1)
                v_evac(3)
                row_max(2)
                pt_evac(1)
                row_max(3)
                v_evac(5)
                row_max(4)
                pt_evac(3)
                row_max(5)
                row_max(6)
                pt_evac(5)
                row_max(7)
                pt_evac(7)
                dve.wait_ge(s["pv_ready"], b * 2 + 2)
                o_ps = PS[:, 6, 0:2 * TP].rearrange("p (g a n) -> p g a n", g=2, a=2)
                step.did(dve.tensor_scalar(oe[:], o_ps[:, :, 0, :], par[:, 0:1], None, ALU.mult))
                step.settle()
                dve.scalar_tensor_tensor(OT[:, :, bass.ds(b * S, S)], o_ps[:, :, 1, :], par[:, 1:2], oe[:],
                                         ALU.mult, ALU.add).then_inc(s["o_done"], 1)
                assert step.n == NPAIR + 1

            d.base = B * (NPAIR + 1)
            pn = [0]

            def post(ins):
                pn[0] += 1
                ins.then_inc(s["dve_post"], 1)

            dve.wait_ge(s["pe_post"], 2)
            rd_v = rd[:].rearrange("p t (i a) -> p t a i", a=2)
            for t in range(TT):
                d.did(dve.tensor_scalar(rd_v[:, t], PS[0:TP, 2, t * H:(t + 1) * H].rearrange("p (a i) -> p a i", a=2), WS, None, ALU.mult))
            d.settle()
            d.did(dve.reciprocal(rd[:], rd[:]))
            d.settle()
            dve.wait_ge(s["pe_post"], 3)
            for t in range(TT):
                o_v = xn[:, t, :].rearrange("p (h j) -> p h j", h=H)
                d.did(dve.tensor_tensor(o_v, PS[0:TP, 3 + t // 2, (t % 2) * D:(t % 2 + 1) * D].rearrange("p (h j) -> p h j", h=H),
                                        rd[:, t, :].unsqueeze(2).to_broadcast([TP, H, DH]), ALU.mult))
            d.settle()
            for t in range(TT):
                d.did(dve.tensor_tensor(xn[:, t, :], xn[:, t, :], bv_r[:], ALU.add))
            post(quantise(xn, TT, am[0:TP], so, xq16))
            dve.wait_ge(s["act_pre"], 9)
            dve.wait_ge(s["pe_post"], 5)
            for t in range(TT):
                d.did(dve.scalar_tensor_tensor(xn[:, t, :], PS[0:TP, 6 + t // 2, (t % 2) * D:(t % 2 + 1) * D], so[:, t:t + 1],
                                               sp_row[:], ALU.mult, ALU.mult))
            d.settle()
            for t in range(TT):
                d.did(dve.tensor_tensor(xn[:, t, :], xn[:, t, :], bp_r[:], ALU.add))
            d.settle()
            for t in range(TT):
                d.did(dve.scalar_tensor_tensor(x1[:, t, :], xn[:, t, :], tg[:, 0:1], x_in[:, t, :], ALU.mult, ALU.add))
            layernorm(x1, xn, 2)
            d.settle()
            post(dve.tensor_scalar(tgf[:], tg[:, 1:2], 1.0 / (FS * FS), None, ALU.mult))
            dve.wait_ge(s["act_post"], 4)
            post(dve.tensor_tensor(xT16[:, 1], xT[:], xT16[:, 0], ALU.subtract))
            logit, e_, z, z2, acc, a, b_, c_ = (r[0], r[1], r[2], r[3], r[4], r[5], r[6], r[7])
            dve.wait_ge(s["pe_post"], 7)
            post(dve.tensor_copy(logit[:], PS[0:TP, 2, 0:TT * E].rearrange("p (t e) -> p t e", t=TT)))
            dve.wait_ge(s["dve_post"], 4)
            post(dve.tensor_scalar(z[:], logit[:], -1.0, None, ALU.mult))
            dve.wait_ge(s["dve_post"], 5)
            post(dve.tensor_tensor(z[:], z[:], logit[:], ALU.min))
            dve.wait_ge(s["act_post"], 5)
            def one(ins):
                d.did(ins)
                d.settle()
            one(dve.tensor_scalar(a[:], e_[:], 2.0, None, ALU.add))
            one(dve.reciprocal(a[:], a[:]))
            one(dve.tensor_tensor(z[:], e_[:], a[:], ALU.mult))
            one(dve.tensor_tensor(z2[:], z[:], z[:], ALU.mult))
            one(dve.tensor_scalar(acc[:], z2[:], 2.0 / 17, 2.0 / 15, ALU.mult, ALU.add))
            for k in (13, 11, 9, 7, 5, 3, 1):
                one(dve.tensor_tensor(acc[:], acc[:], z2[:], ALU.mult))
                one(dve.tensor_scalar(acc[:], acc[:], 2.0 / k, None, ALU.add))
            one(dve.tensor_tensor(acc[:], acc[:], z[:], ALU.mult))
            dve.scalar_tensor_tensor(a[:], logit[:], 0.0, acc[:], ALU.max, ALU.add).then_inc(s["sp_ready"], 1)
            dve.wait_ge(s["act_post"], 6)
            sc, bias = acc, z2
            one(dve.tensor_tensor(bias[:], sc[:], gb_r[:].unsqueeze(1).to_broadcast([TP, TT, E]), ALU.add))
            for k, oh in enumerate((e_, z)):
                one(dve.tensor_reduce(rs[0][:], bias[:], AX.X, ALU.max))
                one(dve.tensor_tensor(a[:], bias[:], rs[0][:].unsqueeze(2).to_broadcast([TP, TT, E]), ALU.is_ge))
                one(dve.tensor_tensor(a[:], a[:], rank[:], ALU.mult))
                one(dve.tensor_reduce(rs[0][:], a[:], AX.X, ALU.max))
                one(dve.tensor_tensor(oh[:], a[:], rs[0][:].unsqueeze(2).to_broadcast([TP, TT, E]), ALU.is_equal))
                one(dve.tensor_tensor(b_[:], sc[:], oh[:], ALU.mult))
                one(dve.tensor_reduce(rs[1 + k][:], b_[:], AX.X, ALU.add))
                if k == 0:
                    one(dve.scalar_tensor_tensor(bias[:], oh[:], -3e38, bias[:], ALU.mult, ALU.add))
            d.did(dve.tensor_tensor(c_[:], e_[:], z[:], ALU.add))
            one(dve.tensor_tensor(rs[3][:], rs[1][:], rs[2][:], ALU.add))
            post(dve.tensor_copy(sel16[:], c_[:]))
            one(dve.reciprocal(rs[3][:], rs[3][:]))
            for k, oh in enumerate((e_, z)):
                one(dve.tensor_tensor(rs[1 + k][:], rs[1 + k][:], rs[3][:], ALU.mult))
                one(dve.tensor_tensor(oh[:], oh[:], rs[1 + k][:].unsqueeze(2).to_broadcast([TP, TT, E]), ALU.mult))
            one(dve.tensor_tensor(a[:], e_[:], z[:], ALU.add))
            dve.wait_ge(s["pe_post"], 8)
            one(dve.tensor_scalar(b_[:], PS[0:TP, 3, 0:TT * E].rearrange("p (t e) -> p t e", t=TT), CAP - 0.5, 0.5 / FS, ALU.is_lt, ALU.mult))
            d.did(dve.tensor_tensor(WT[:, 0:E * TT].rearrange("p (e t) -> p t e", t=TT), a[:], b_[:], ALU.mult))
            d.settle()
            post_steps = d.n

            def weights_lo(q, n):
                dve.wait_ge(s["wh_done"], n)
                dve.scalar_tensor_tensor(w13T[q][:, 1], PS[:, 4:6, 0:2 * I], FS, w13T[q][:, 0], ALU.mult, ALU.subtract)
                dve.scalar_tensor_tensor(w2T[q][:, 1], PS[0:IH, 6, :], FS, w2T[q][:, 0], ALU.mult, ALU.subtract).then_inc(s["wl_done"], 1)

            def expert(e, q, prepare):
                own = Steps(dve, s["dve_step"], e * (TT + 1) + (d.base + post_steps))
                own.did(dve.tensor_copy(wcur[:, q, :], WT[:, bass.ds(e * TT, TT)]))

                def hidden(t):
                    dve.wait_ge(s["tanh_done"], e * TT + t + 1)
                    own.did(dve.scalar_tensor_tensor(hg[:, t % 2, :], th[:, t % 2, :], 1.0, PS[0:TP, 2 + t % 2, 0:I], ALU.add, ALU.mult))
                    own.settle()
                    dve.scalar_tensor_tensor(hn[:, t, :], PS[0:TP, 2 + t % 2, I:2 * I], wcur[:, q, t:t + 1], hg[:, t % 2, :],
                                             ALU.mult, ALU.mult).then_inc(s["h_done"], 1)

                def h_lo(p):
                    dve.wait_ge(s["hh_done"], e * 2 + p + 1)
                    dve.tensor_tensor(hT[:, 1, p, :], PS[0:IH, 7, 0:4 * TP], hT[:, 0, p, :], ALU.subtract).then_inc(s["hl_done"], 1)

                dve.wait_ge(s["ht_ready"], e * 2)
                hidden(0)
                hidden(1)
                hidden(2)
                h_lo(0)
                hidden(3)
                if prepare:
                    weights_lo(1 - q, e + 2)
                h_lo(1)
                assert own.n == TT + 1

            weights_lo(0, 1)
            with dve.Fori(0, E // 2) as it:
                for q in range(2):
                    expert(it * 2 + q, q, True)
            expert(E, 0, False)
            dve.wait_ge(s["y_ready"], 2 * (E + 1))
            for t in range(TT):
                last = dve.scalar_tensor_tensor(y_out[:, t, :], PS[0:TP, t // 2, (t % 2) * D:(t % 2 + 1) * D], tgf[:, 0:1], x1[:, t, :],
                                                ALU.mult, ALU.add)
            last.then_inc(s["y_final"], 1)

        @block.tensor
        def _(pe):
            mm, tp = pe.matmul, pe.transpose

            def split3(out_, w, x_, first=True, last=True, halves=2):
                todo = [(a, b, h) for a, b in SPLIT for h in range(halves)]
                for k, (a, b, h) in enumerate(todo):
                    ins = mm(out_, w(a, h), x_(b, h), start=first and k == 0, stop=last and k == len(todo) - 1)
                return ins

            pe.wait_ge(s["consts"], NCONST)
            pe.wait_ge(s["wkv_loaded"], 16)
            for h in range(NH):
                for k in range(2 * NH):
                    last = tp(PS[:, h, k * 128:(k + 1) * 128], wkv_in[:, k, h * 128:(h + 1) * 128], ident[:])
            last.then_inc(s["pe_pre"], 1)
            pe.wait_ge(s["xq_ready"], 1)
            for h in range(NH):
                for t in range(TT):
                    last = tp(bank16(2)[:, h * T + t * TP:h * T + (t + 1) * TP], xq16[:, t, h * 128:(h + 1) * 128], ident16[0:TP, 0:TP])
            last.then_inc(s["pe_pre"], 1)
            pe.wait_ge(s["wqq_ready"], 1)
            for h in range(NH):
                for k in range(NH):
                    last = tp(bank16(3)[:, h * D + k * 128:h * D + (k + 1) * 128], wq16[:, k, h * 128:(h + 1) * 128], ident16[:])
            last.then_inc(s["pe_pre"], 1)
            pe.wait_ge(s["sx_diag"], 1)
            for t in range(TT):
                last = mm(PS[:, 5, t * TP:(t + 1) * TP], ones[0:TP, :], diag[0:TP, t, 0:TP], start=True, stop=True)
            last.then_inc(s["pe_pre"], 1)
            pe.wait_ge(s["act_pre"], 5)
            for k in range(NH):
                for h in range(NH):
                    last = mm(PS[:, 6 + k, 0:T], wqT[:, h, k * 128:(k + 1) * 128], xqT[:, h, :], start=h == 0, stop=h == NH - 1)
            last.then_inc(s["pe_pre"], 1)
            pe.wait_ge(s["wpq_ready"], 1)
            for h in range(NH):
                for k in range(NH):
                    last = tp(bank16(4)[:, h * D + k * 128:h * D + (k + 1) * 128], wp16[:, k, h * 128:(h + 1) * 128], ident16[:])
            last.then_inc(s["pe_pre"], 1)
            pe.wait_ge(s["sp_diag"], 1)
            for k in range(NH):
                last = mm(PS[0:TP, 3, k * 128:(k + 1) * 128], ones[:, 0:TP], diag[:, k, :], start=True, stop=True)
            last.then_inc(s["pe_pre"], 1)
            pe.wait_ge(s["small_loaded"], NSMALL)
            for h in range(NH):
                last = tp(PS[:, 2, h * E:(h + 1) * E], gate_in[:, h * 128:(h + 1) * 128], ident[0:E, 0:E])
            last.then_inc(s["pe_pre"], 1)
            pe.wait_ge(s["act_pre"], 9)
            pe.wait_ge(s["dve_pre"], 1)
            pe.wait_ge(s["qs_ready"], 1)

            with pe.Fori(0, B) as b:
                pe.wait_ge(s["pt_act"], b * 4)
                pe.wait_ge(s["pt_dve"], b * 4)
                for u in range(6):
                    c, hf = divmod(u, 2)
                    if hf == 0:
                        pe.wait_ge(ctx_in[c], b * 16 + 16)
                    for j in range(4):
                        last = tp(PS[:, u, j * KP:(j + 1) * KP], c_in[:, 4 * c + j, hf * 128:(hf + 1) * 128], ident[0:KP, 0:KP])
                    last.then_inc(s["t_ready"], 1)
                for u in range(6):
                    c, oh = divmod(u, 2)
                    pe.wait_ge(s["tl_done"], b * 6 + max(2 * c + 2, u + 1))
                    split3(PS[:, u, 0:CW], lambda a, h: wkvT[:, a, h, oh * 128:(oh + 1) * 128],
                           lambda a, h: cT[:, a, h, c * CW:(c + 1) * CW]).then_inc(s["k_ready"], 1)

                def scores(i):
                    if i == 0:
                        pe.wait_ge(s["kl_done"], b * 6 + 6)
                        pe.wait_ge(s["qc_done"], b + 1)
                    elif i >= 2:
                        pe.wait_ge(s["pt_dve" if i % 2 else "pt_act"], b * 4 + (i - 2) // 2 + 1)
                    g, j = divmod(i, 2)
                    for k in range(2):
                        for c in range(CH):
                            last = mm(PS[0:TP, 3 * (i % 2) + c, 0:CW], QC[:, (g * 2 + k) * 4 * S + j * TP:(g * 2 + k) * 4 * S + (j + 1) * TP],
                                      KS[:, g, c * CW:(c + 1) * CW], start=k == 0, stop=k == 1)
                    last.then_inc(s["sc_ready"], 1)

                def values(v):
                    if v == 0:
                        pe.wait_ge(s["o_done"], b)
                        pe.wait_ge(s["v_dve"], b * 3)
                    elif v >= 2:
                        pe.wait_ge(s["v_dve" if v % 2 else "v_act"], b * 3 + (v - 2) // 2 + 1)
                    for k in range(2):
                        t = 2 * v + k
                        last = split3(PS[0:KP, 6 + v % 2, k * D:(k + 1) * D], lambda a, h: cT[:, a, h, t * KP:(t + 1) * KP],
                                      lambda a, h: wkvT[:, a, h, D:2 * D])
                    last.then_inc(s["v_ready"], 1)

                def turn(i):
                    pe.wait_ge(s["exp_done"], b * NPAIR + i + 1)
                    for t in range(KT):
                        last = tp(PS[0:KP, 3 * (i % 2) + t // 4, (t % 4) * TP:(t % 4 + 1) * TP], P[:, i % 2, t * KP:(t + 1) * KP],
                                  ident[0:TP, 0:TP])
                    last.then_inc(s["tr_ready"], 1)

                def outputs(gh, t0, t1):
                    if t0 == 0:
                        pe.wait_ge(s["pt_act"], b * 4 + 2 * gh + 2)
                        pe.wait_ge(s["pt_dve"], b * 4 + 2 * gh + 2)
                        pe.wait_ge(s["v_act"], b * 3 + 3)
                        pe.wait_ge(s["v_dve"], b * 3 + 3)
                    for t in range(t0, t1):
                        for j in range(4):
                            i = 4 * gh + j
                            last = mm(PS[32 * j:32 * j + 32, 6, gh * TP:(gh + 1) * TP], V[:, t, i * 32:(i + 1) * 32],
                                      PT[:, i, t * TP:(t + 1) * TP], start=t == 0, stop=t == KT - 1,
                                      tile_position=(0, 32 * j))
                    if t1 == KT:
                        last.then_inc(s["pv_ready"], 1)

                scores(0)
                values(0)
                values(1)
                scores(1)
                values(2)
                turn(0)
                values(3)
                scores(2)
                turn(1)
                values(4)
                scores(3)
                turn(2)
                values(5)
                scores(4)
                turn(3)
                scores(5)
                turn(4)
                outputs(0, 0, 4)
                scores(6)
                turn(5)
                outputs(0, 4, 8)
                scores(7)
                turn(6)
                outputs(0, 8, KT)
                turn(7)
                outputs(1, 0, KT)

            pe.wait_ge(s["den_saved"], B)
            pe.wait_ge(s["o_done"], B)
            pe.wait_ge(s["pt_act"], 4 * B)
            pe.wait_ge(s["pt_dve"], 4 * B)
            for k in range(B):
                last = tp(PS[0:NPAIR, k // 4, (k % 4) * TP:(k % 4 + 1) * TP], den_all[:, k * NPAIR:(k + 1) * NPAIR], ident[0:TP, 0:TP])
            last.then_inc(s["pe_post"], 1)
            pe.wait_ge(s["act_post"], 1)
            dT_v = dT[:].rearrange("p (a k) -> p a k", a=2)
            for t in range(TT):
                for a in range(2):
                    last = tp(PS[0:TP, 2, t * H + a * NPAIR:t * H + (a + 1) * NPAIR], dT_v[:, a, t * TP:(t + 1) * TP], ident[0:NPAIR, 0:NPAIR])
            last.then_inc(s["pe_post"], 1)
            for t in range(TT):
                for g in range(2):
                    last = tp(PS[0:TP, 3 + t // 2, (t % 2) * D + g * 128:(t % 2) * D + (g + 1) * 128], OT[:, g, t * TP:(t + 1) * TP], ident[:])
            last.then_inc(s["pe_post"], 1)
            pe.wait_ge(s["dve_post"], 1)
            for h in range(NH):
                for t in range(TT):
                    last = tp(bank16(5)[:, h * T + t * TP:h * T + (t + 1) * TP], xq16[:, t, h * 128:(h + 1) * 128], ident16[0:TP, 0:TP])
            last.then_inc(s["pe_post"], 1)
            pe.wait_ge(s["act_post"], 2)
            for t in range(TT):
                for h in range(NH):
                    last = mm(PS[0:TP, 6 + t // 2, (t % 2) * D:(t % 2 + 1) * D], xqT[:, h, t * TP:(t + 1) * TP], wpT[:, h, :], start=h == 0, stop=h == NH - 1)
            last.then_inc(s["pe_post"], 1)
            pe.wait_ge(s["dve_post"], 2)
            for h in range(NH):
                for t in range(TT):
                    last = tp(PS[:, h, t * TP:(t + 1) * TP], xn[:, t, h * 128:(h + 1) * 128], ident[0:TP, 0:TP])
            last.then_inc(s["pe_post"], 1)

            def weights(q, n):
                pe.wait_ge(w_in[q], ((n + 1) // 2) * 48 if isinstance(n, int) else n)
                for h in range(NH):
                    for k in range(4):
                        tp(PS[:, 4 + h, k * IH:(k + 1) * IH], w13_in[q][:, k, h * 128:(h + 1) * 128], ident[0:IH, 0:IH])
                for k in range(2):
                    for h in range(NH):
                        last = tp(PS[0:IH, 6, k * D + h * 128:k * D + (h + 1) * 128], w2_in[q][:, h, k * IH:(k + 1) * IH], ident[:])
                last.then_inc(s["wt_ready"], 1)

            pe.wait_ge(s["act_post"], 4)
            for t in range(TT):
                for h in range(NH):
                    last = mm(PS[0:TP, 2, t * E:(t + 1) * E], xT[:, h, t * TP:(t + 1) * TP], gateT[:, h, :], start=h == 0, stop=h == NH - 1)
            last.then_inc(s["pe_post"], 1)
            weights(0, 1)
            for k in range(2):
                mm(PS[0:TP, k, :], zero16[:, 0:TP], zero16[:], start=True, stop=False, skip_group_check=True)
            pe.wait_ge(s["dve_post"], 7)
            for t in range(TT):
                for k in range(t + 1):
                    last = mm(PS[0:TP, 3, t * E:(t + 1) * E], (before16 if k == t else ones16)[:], sel16[:, k, :],
                              start=k == 0, stop=k == t)
            last.then_inc(s["pe_post"], 1)
            pe.wait_ge(s["dve_post"], 7)

            def expert(e, q, prepare, final=False):
                def gate_up(t):
                    pe.wait_ge(s["h_done"], e * TT + max(t - 1, 0))
                    split3(PS[0:TP, 2 + t % 2, 0:2 * I], lambda a, h: xT16[:, a, h, t * TP:(t + 1) * TP],
                           lambda a, h: w13T[q][:, a, h, :]).then_inc(s["gu_ready"], 1)

                def turn_h(p):
                    pe.wait_ge(s["h_done"], e * TT + 2 * p + 2)
                    pe.wait_ge(s["hl_done"], e * 2 + p)
                    for k in range(2):
                        for t in range(2):
                            last = tp(PS[0:IH, 7, (k * 2 + t) * TP:(k * 2 + t + 1) * TP], hn[:, 2 * p + t, k * IH:(k + 1) * IH], ident[0:TP, 0:TP])
                    last.then_inc(s["ht_ready"], 1)

                def down(p):
                    pe.wait_ge(s["hl_done"], e * 2 + p + 1)
                    for t in range(2):
                        todo = [(a, b, k) for a, b in SPLIT for k in range(2)]
                        for n, (a, b, k) in enumerate(todo):
                            last = mm(PS[0:TP, p, t * D:(t + 1) * D], hT[:, a, p, (k * 2 + t) * TP:(k * 2 + t + 1) * TP],
                                      w2T[q][:, b, k * D:(k + 1) * D], start=False, stop=final and n == len(todo) - 1,
                                      skip_group_check=True)
                    last.then_inc(s["y_ready"], 1)

                pe.wait_ge(s["wl_done"], e + 1)
                gate_up(0)
                gate_up(1)
                gate_up(2)
                turn_h(0)
                gate_up(3)
                down(0)
                if prepare is not None:
                    weights(1 - q, prepare)
                turn_h(1)
                down(1)

            pe.wait_ge(s["dve_post"], 3)

            with pe.Fori(0, E // 2) as it:
                expert(it * 2, 0, it * 48 + 48)
                expert(it * 2 + 1, 1, it * 48 + 96)
            expert(E, 0, None, final=True)


_INS = ["x", "ctx_2048", "g_xattn", "g_ffn", "L0_xattn_wq", "L0_xattn_bq", "L0_xattn_wkv", "L0_xattn_bkv",
        "L0_xattn_wp", "L0_xattn_bp", "L0_ffn_gate_w", "L0_ffn_gate_b", "L0_ffn_W1", "L0_ffn_W3", "L0_ffn_W2",
        "L0_ffn_Ws1", "L0_ffn_Ws3", "L0_ffn_Ws2"]


def kernel(**inputs):
    import numpy as np
    import concourse.bacc as bacc
    from concourse.bass_utils import run_bass_kernel_spmd

    nc = bacc.Bacc("TRN2", target_bir_lowering=False, num_devices=1)
    arrays, args = {}, []
    for name in _INS:
        a = np.ascontiguousarray(inputs[name])
        arrays[name] = a
        args.append(nc.dram_tensor(name, a.shape, mybir.dt.from_np(a.dtype), kind="ExternalInput").ap())
    args.append(nc.dram_tensor("y", (B, S, D), F32, kind="ExternalOutput").ap())
    program(nc, *args)
    return run_bass_kernel_spmd(nc, [arrays], core_ids=[0]).results[0]["y"]
```

```python
import concourse.bass as bass
from concourse import mybir
from contextlib import ExitStack

F32 = mybir.dt.float32
F16 = mybir.dt.float16
ALU = mybir.AluOpType
ACT = mybir.ActivationFunctionType
AX = mybir.AxisListType

B, S, D = 8, 56, 256
M = 1500
H, DH = 16, 16
E, I = 16, 176
CAP = 128
T = B * S
TP, TT = 112, 4
NH = D // 128
KP, KT = 125, 12
CH = 3
CW = M // CH
G = 4
NPAIR = H // 2
QW = G * 2 * 4 * S
IH = I // 2
WS = 64.0
FS = 16.0
SCORE = DH ** -0.5 / WS
MAGIC = 1.5 * 2.0 ** 23
EPS = 1e-5
NCONST = 17
NSMALL = 8 * 16
SEQ_STEPS = 4 * NPAIR + 2
WP_STEPS = 4 + NH
SCN = NPAIR * CH
SPLIT = ((0, 0), (0, 1), (1, 0))


class Steps:

    def __init__(self, eng, sem, base=0):
        self.eng, self.sem, self.base, self.n = eng, sem, base, 0

    def did(self, ins):
        ins.then_inc(self.sem, 1)
        self.n += 1

    def settle(self):
        self.eng.wait_ge(self.sem, self.base + self.n)


def program(nc, x, ctx, g_xattn, g_ffn, wq, bq, wkv, bkv, wp, bp, gate_w, gate_b, W1, W3, W2, Ws1, Ws3, Ws2, out):
    stack = ExitStack()
    with stack:
        def sb(name, shape, dt=F32):
            return stack.enter_context(nc.sbuf_tensor(name, shape, dt))

        def sem(name):
            return stack.enter_context(nc.semaphore(name))

        ident = sb("ident", [128, 128])
        ident16 = sb("ident16", [128, 128], F16)
        ones = sb("ones", [128, 128])
        ones16 = sb("ones16", [TP, TP], F16)
        before16 = sb("before16", [TP, TP], F16)
        hm2 = sb("hm2", [128, 2, 4])
        hmask = sb("hmask", [128, 4])
        par = sb("par", [128, 2])
        rank = sb("rank", [TP, TT, E])
        x_in = sb("x_in", [TP, TT, D])
        wq_in = sb("wq_in", [128, NH, D])
        wp_in = sb("wp_in", [128, NH, D])
        wkv_in = sb("wkv_in", [128, 2 * NH, D])
        gate_in = sb("gate_in", [E, D])
        bq_c = sb("bq_c", [128, NH])
        bk_c = sb("bk_c", [128, NH])
        bv_r = sb("bv_r", [TP, D])
        bp_r = sb("bp_r", [TP, D])
        gb_r = sb("gb_r", [TP, E])
        gx = sb("gx", [TP, 2])
        tg = sb("tg", [TP, 2])
        tgf = sb("tgf", [TP, 1])
        st = sb("st", [TP, TT, 6])
        mv = sb("mv", [TP, TT, 2])
        var = sb("var", [TP, TT])
        mhalf = sb("mhalf", [TP, TT])
        rstd = sb("rstd", [TP, TT])
        am = sb("am", [128, TT])
        sx = sb("sx", [TP, TT])
        swq = sb("swq", [128, NH])
        swp = sb("swp", [128, NH])
        so = sb("so", [TP, TT])
        xn = sb("xn", [TP, TT, D])
        xq16 = sb("xq16", [TP, TT, D], F16)
        wq16 = sb("wq16", [128, NH, D], F16)
        wp16 = sb("wp16", [128, NH, D], F16)
        wqT = sb("wqT", [128, NH, D], F16)
        wpT = sb("wpT", [128, NH, D], F16)
        xqT = sb("xqT", [128, NH, T], F16)
        diag = sb("diag", [128, TT, 128])
        sx_row = sb("sx_row", [128, T])
        sp_row = sb("sp_row", [TP, D])
        qT = sb("qT", [128, NH, T])
        LATE = 2 * (NH * T + 2 * 2 * NH * I + 2 * 2 * D + 2 * TT * TP)
        shared = sb("shared", [128, LATE], F16)
        q16 = shared[:, 0:G * 2 * T].rearrange("p (g k t) -> p g k t", g=G, k=2)
        QC = sb("QC", [128, QW], F16)
        hmask16 = sb("hmask16", [128, 4], F16)
        wkvT = sb("wkvT", [128, 2, NH, 2 * D], F16)
        c_in = sb("c_in", [KP, KT, D])
        cT = sb("cT", [128, 2, NH, M], F16)
        KS = sb("KS", [128, G, M], F16)
        V = sb("V", [KP, KT, D])
        P = sb("P", [TP, 2, M])
        PT_all = sb("PT_all", [128, NPAIR, KT * TP])
        PT = PT_all[0:KP]
        qd = PT_all[:, 0:2, 0:2 * T].rearrange("p a (b t) -> p a b t", b=2)
        hn, th, hg = (PT_all[0:TP, k, 0:TT * I].rearrange("p (t i) -> p t i", t=TT) for k in (4, 5, 6))
        mx = sb("mx", [TP, NPAIR, 4])
        nmx = sb("nmx", [TP, NPAIR])
        den = sb("den", [TP, NPAIR])
        den_all = sb("den_all", [TP, B * NPAIR])
        oe = sb("oe", [128, 2, S])
        OT = sb("OT", [128, 2, T])
        dT = sb("dT", [NPAIR, B * TP])
        rd = sb("rd", [TP, TT, H])
        x1 = sb("x1", [TP, TT, D])
        xT = qT
        at = [0]

        def over_queries(rows, *shape):
            n = 1
            for k in shape:
                n *= k
            at[0] += n
            assert at[0] <= LATE
            names = "abc"[:len(shape)]
            return shared[0:rows, at[0] - n:at[0]].rearrange(
                f"p ({' '.join(names)}) -> p {' '.join(names)}", **dict(zip(names, shape)))

        xT16 = over_queries(128, 2, NH, T)
        gateT = sb("gateT", [128, NH, E])
        r = [sb(f"r{i}", [TP, TT, E]) for i in range(8)]
        rs = [sb(f"rs{i}", [TP, TT]) for i in range(5)]
        sel16 = sb("sel16", [TP, TT, E], F16)
        WT = sb("WT", [TP, (E + 1) * TT])
        wcur = sb("wcur", [TP, 2, TT])
        zero16 = sb("zero16", [TP, 512], F16)
        w13_in = [sb(f"w13_in{i}", [IH, 4, D]) for i in range(2)]
        w2_in = [sb(f"w2_in{i}", [128, NH, I]) for i in range(2)]
        w13T = [over_queries(128, 2, NH, 2 * I) for i in range(2)]
        w2T = [over_queries(IH, 2, 2 * D) for i in range(2)]
        hT = over_queries(IH, 2, 2, 2 * 2 * TP)
        y_out = xn

        PS = stack.enter_context(nc.psum_tensor("PS", [128, 8, 512], F32))

        def bank16(b):
            return PS[:, b, :].bitcast(F16)

        names = """consts var_ready rstd_ready sp_ready x_loaded wq_loaded wp_loaded wkv_loaded small_loaded xq_ready wqq_ready wpq_ready
            sx_diag sp_diag pe_pre act_pre dve_pre qs_ready dve_step
            t_ready th_done tl_done k0_ready kh0_done kl0_done k1_ready kh1_done kl1_done
            qc0_done qc1_done sc_ready max_done exp_done tr_ready pt_act pt_dve v_ready v_act pv_ready o_done den_saved
            pe_post act_post dve_post pe_weights act_weights
            wt_ready wh_done w13l_done wl_done gu_ready tanh_done h_done ht_ready hh_done hl_done y_ready
            y_final stored""".split()
        s = {n: sem(n) for n in names}
        credited = names[names.index("t_ready"):names.index("den_saved") + 1] + names[names.index("wt_ready"):names.index("y_ready") + 1]

        def after(eng, name, n):
            eng.wait_ge(s[name], n + 1)

        ctx_in = [sem(f"ctx_in{c}") for c in range(CH)]
        w_in = [sem(f"w_in{i}") for i in range(2)]

        ctx_v = ctx.rearrange("b (p t) d -> b p t d", t=KT)
        w13_v = [w.rearrange("e (r p) d -> e p r d", p=IH) for w in (W1, W3)]
        w2_v = W2.rearrange("e (r p) i -> e p r i", p=128)
        v_bank = (7, 6, 7, 6, 7, 6)
        t_bank = (6, 7, 6, 7, 6, 7)
        t0_bank = (2, 3, 4, 5, 6, 0)
        k0_bank = (4, 5, 6)
        k_bank = ((7, 6, 7), (6, 7, 6))
        o_bank = (6, 7)
        g_bank = (2, 3, 6, 2)
        h_bank = (7, 2)
        order = (2, 0, 1)
        block = stack.enter_context(nc.Block())

        @block.sync
        def _(sp):
            sp.dma_start(x_in[:], x.rearrange("b s d -> (b s) d").rearrange("(t p) d -> p t d", p=TP)).then_inc(s["x_loaded"], 16)
            sp.dma_start(wkv_in[:], wkv.rearrange("(r p) d -> p r d", p=128)).then_inc(s["wkv_loaded"], 16)
            for c in range(CH):
                sp.dma_start(c_in[:, 4 * c:4 * c + 4, :], ctx_v[0, :, 4 * c:4 * c + 4, :]).then_inc(ctx_in[c], 16)
                if c == 0:
                    sp.dma_start(wq_in[:], wq.rearrange("(r p) d -> p r d", p=128)).then_inc(s["wq_loaded"], 16)
            sp.dma_start(wp_in[:], wp.rearrange("(r p) d -> p r d", p=128)).then_inc(s["wp_loaded"], 16)
            with sp.Fori(1, B) as b:
                for c in range(CH):
                    after(sp, "t_ready", b * 6 + (2 * c + 2 - 6))
                    sp.dma_start(c_in[:, 4 * c:4 * c + 4, :], ctx_v[b, :, 4 * c:4 * c + 4, :]).then_inc(ctx_in[c], 16)

            def load(e, q, srcs):
                for k in range(2):
                    sp.dma_start(w13_in[q][:, 2 * k:2 * k + 2, :], srcs[k]).then_inc(w_in[q], 16)
                sp.dma_start(w2_in[q][:], srcs[2]).then_inc(w_in[q], 16)

            for e in range(2):
                load(e, e, (w13_v[0][e], w13_v[1][e], w2_v[e]))
            with sp.Fori(1, E // 2) as it:
                for q in range(2):
                    after(sp, "wt_ready", it * 2 + (q - 1))
                    load(None, q, (w13_v[0][it * 2 + q], w13_v[1][it * 2 + q], w2_v[it * 2 + q]))
            after(sp, "wt_ready", E - 1)
            load(E, 0, (Ws1.rearrange("(r p) d -> p r d", p=IH), Ws3.rearrange("(r p) d -> p r d", p=IH),
                        Ws2.rearrange("(r p) i -> p r i", p=128)))
            sp.wait_ge(s["y_final"], 1)
            sp.dma_start(out.rearrange("b s d -> (b s) d").rearrange("(t p) d -> p t d", p=TP), y_out[:]).then_inc(s["stored"], 16)
            sp.wait_ge(s["stored"], 16)

        @block.gpsimd
        def _(gp):
            for name in credited:
                gp.sem_inc(s[name], 1)
            c = Steps(gp, s["consts"])
            for t, v in ((ident, 0.0), (ident16, 0.0), (ones, 1.0), (ones16, 1.0), (before16, 1.0), (hm2, 1.0),
                         (zero16, 0.0), (mhalf, -0.5)):
                c.did(gp.memset(t[:], v))
            c.did(gp.iota(rank[:], [[0, TT], [-1, E]], base=E, channel_multiplier=0, allow_small_or_imprecise_dtypes=True))
            c.did(gp.memset(WT[:, E * TT:], 0.5 / FS))
            c.settle()
            for t in (ident, ident16):
                c.did(gp.affine_select(out=t[:], in_=t[:], compare_op=ALU.not_equal, fill=1.0, base=0,
                                       pattern=[[-1, 128]], channel_multiplier=1))
            c.did(gp.affine_select(out=before16[:], in_=before16[:], compare_op=ALU.is_ge, fill=0.0, base=-1,
                                   pattern=[[1, TP]], channel_multiplier=-1))
            c.did(gp.affine_select(out=hm2[:], in_=hm2[:], compare_op=ALU.is_ge, fill=0.0, base=0,
                                   pattern=[[-64, 2], [-16, 4]], channel_multiplier=1))
            c.settle()
            c.did(gp.affine_select(out=hm2[:], in_=hm2[:], compare_op=ALU.is_ge, fill=0.0, base=DH - 1,
                                   pattern=[[64, 2], [16, 4]], channel_multiplier=-1))
            c.settle()
            c.did(gp.tensor_tensor(hmask[:], hm2[:, 0, :], hm2[:, 1, :], ALU.add))
            c.settle()
            c.did(gp.tensor_tensor(par[:], hmask[:, 0:2], hmask[:, 2:4], ALU.add))
            c.did(gp.tensor_copy(hmask16[:], hmask[:]))
            c.settle()
            gp.wait_ge(s["var_ready"], 1)
            gp.tensor_tensor(rstd[:], var[:], mhalf[:], ALU.pow).then_inc(s["rstd_ready"], 1)
            gp.wait_ge(s["qs_ready"], 1)

            def queries(n, k):
                own = q16.rearrange("p g k t -> p (g k) t")[:, 4 * k:4 * k + 4, bass.ds(n * S, S)]
                gp.tensor_tensor(QC[:, k * (QW // 2):(k + 1) * (QW // 2)].rearrange("p (c h n) -> p c h n", c=4, h=4),
                                 own.unsqueeze(2).to_broadcast([128, 4, 4, S]),
                                 hmask16[:].unsqueeze(1).unsqueeze(3).to_broadcast([128, 4, 4, S]), ALU.mult).then_inc(s[f"qc{k}_done"], 1)

            def sums(b):
                after(gp, "exp_done", b * NPAIR + NPAIR)
                gp.tensor_copy(den_all[:, bass.ds(b * NPAIR, NPAIR)], den[:]).then_inc(s["den_saved"], 1)

            for k in range(2):
                queries(0, k)
            with gp.Fori(0, B - 1) as b:
                for k in range(2):
                    after(gp, "sc_ready", b * SCN + (k + 1) * (SCN // 2))
                    queries(b + 1, k)
                sums(b)
            sums(B - 1)
            gp.wait_ge(s["var_ready"], 2)
            gp.tensor_tensor(rstd[:], var[:], mhalf[:], ALU.pow).then_inc(s["rstd_ready"], 1)


        @block.scalar
        def _(act):
            for t, src in ((bq_c, bq.rearrange("(r p) -> p r", p=128)), (bk_c, bkv[0:D].rearrange("(r p) -> p r", p=128)),
                           (bv_r, bkv[D:2 * D].partition_broadcast(TP)), (bp_r, bp.partition_broadcast(TP)),
                           (gb_r, gate_b.partition_broadcast(TP))):
                act.dma_start(t[:], src, allow_slow_non_contiguous=True).then_inc(s["small_loaded"], 16)
            act.dma_start(gate_in[:], gate_w).then_inc(s["small_loaded"], 16)
            for k, g in enumerate((g_xattn, g_ffn)):
                act.dma_start(gx[:, k:k + 1], g.partition_broadcast(TP)).then_inc(s["small_loaded"], 16)
            ap = Steps(act, s["act_pre"])
            act.wait_ge(s["pe_pre"], 1)
            ap.did(act.activation(wkvT[:, 0], PS[:, 0:2, :], ACT.Copy, scale=WS))

            def context_hi(n, u, b=None):
                c, hf = divmod(u, 2)
                bank = (t0_bank if b is None else t_bank)[u]
                after(act, "t_ready", n * 6 + u + 1)
                if b is not None and hf == 0:
                    after(act, "v_ready", b * 6 + 2 * c + 2)
                    after(act, "k1_ready", b * 3 + c + 1)
                act.activation(cT[:, 0, hf, c * CW:(c + 1) * CW], PS[:, bank, 0:CW], ACT.Copy).then_inc(s["th_done"], 1)

            def keys_hi(n, oh, c, bank=None):
                after(act, f"k{oh}_ready", n * 3 + c + 1)
                if c == 0 and bank is None:
                    after(act, "sc_ready", n * SCN - (SCN // 2 if oh == 0 else 0))
                for k in range(2):
                    rows = slice(64 * k, 64 * k + 64)
                    act.activation(KS[rows, 2 * oh + k, c * CW:(c + 1) * CW], PS[rows, bank or k_bank[oh][c], 0:CW], ACT.Identity,
                                   bias=bk_c[rows, oh:oh + 1]).then_inc(s[f"kh{oh}_done"], 1)

            def act_sequence(b, prepare):
                n = b + 1

                def v_evac(v):
                    after(act, "v_ready", b * 6 + v + 1)
                    act.activation(V[:, 2 * v:2 * v + 2, :].rearrange("p t d -> p (t d)"), PS[0:KP, v_bank[v], :],
                                   ACT.Copy).then_inc(s["v_act"], 1)

                def exp(i):
                    after(act, "max_done", b * NPAIR + i + 1)
                    after(act, "tr_ready", b * NPAIR + max(i - 1, 0))
                    act.activation(P[:, i % 2, :].rearrange("p (c k) -> p c k", c=CH),
                                   PS[0:TP, 3 * (i % 2):3 * (i % 2) + 3, 0:CW], ACT.Exp, bias=nmx[:, i:i + 1],
                                   scale=SCORE, accum_out=den[:, i:i + 1]).then_inc(s["exp_done"], 1)

                def pt_evac(i):
                    after(act, "tr_ready", b * NPAIR + i + 1)
                    act.activation(PT[:, i, 0:8 * TP].rearrange("p (c k) -> p c k", c=2),
                                   PS[0:KP, 3 * (i % 2):3 * (i % 2) + 2, 0:4 * TP], ACT.Copy).then_inc(s["pt_act"], 1)

                def next_context(*units):
                    if prepare:
                        for u in units:
                            context_hi(n, u, b)

                def next_keys(c):
                    if prepare:
                        keys_hi(n, 0, c)

                keys_hi(b, 1, 0)
                after(act, "pv_ready", b * 2)
                v_evac(0)
                after(act, "den_saved", b)
                exp(0)
                keys_hi(b, 1, 1)
                pt_evac(0)
                v_evac(1)
                exp(1)
                keys_hi(b, 1, 2)
                pt_evac(1)
                exp(2)
                v_evac(2)
                next_context(0)
                pt_evac(2)
                next_context(1)
                exp(3)
                next_keys(0)
                pt_evac(3)
                exp(4)
                v_evac(3)
                v_evac(4)
                next_context(2)
                exp(5)
                next_context(3)
                pt_evac(4)
                v_evac(5)
                pt_evac(5)
                next_context(4, 5)
                exp(6)
                next_keys(1)
                exp(7)
                pt_evac(6)
                next_keys(2)
                pt_evac(7)

            for u in range(5):
                context_hi(0, u)
            act.wait_ge(s["small_loaded"], NSMALL)
            ap.did(act.activation(tg[:, 0:1], gx[:, 0:1], ACT.Tanh))
            ap.did(act.activation(bk_c[:], bk_c[:], ACT.Copy, scale=WS))
            act.wait_ge(s["pe_pre"], 2)
            ap.did(act.activation(xqT[:], bank16(7)[:, 0:NH * T].rearrange("p (h t) -> p h t", h=NH), ACT.Copy))
            act.wait_ge(s["pe_pre"], 3)
            ap.did(act.activation(sx_row[:], PS[:, 1, 0:T], ACT.Copy))
            context_hi(0, 5)
            act.wait_ge(s["pe_pre"], 4)
            ap.did(act.activation(wqT[:], bank16(7)[:, 0:NH * D].rearrange("p (h t) -> p h t", h=NH), ACT.Copy))
            act.wait_ge(s["act_pre"], 3)
            for c in range(CH):
                keys_hi(0, 0, c, bank=k0_bank[c])
            with act.Fori(0, B - 1) as b:
                act_sequence(b, True)
            act_sequence(B - 1, False)

            act.wait_ge(s["pe_post"], 1)
            dT_w = dT[:].rearrange("p (a b n) -> p b a n", a=2, b=B)
            for k in range(2):
                last = act.activation(dT_w[:, 4 * k:4 * k + 4], PS[0:NPAIR, k, 0:4 * TP].rearrange("p (b a n) -> p b a n", b=4, a=2), ACT.Copy)
            last.then_inc(s["act_post"], 1)
            act.wait_ge(s["pe_weights"], 1)
            act.activation(wpT[:], bank16(5)[:, 0:NH * D].rearrange("p (h t) -> p h t", h=NH), ACT.Copy).then_inc(s["act_weights"], 1)
            act.wait_ge(s["pe_weights"], 2)
            act.activation(sp_row[:], PS[0:TP, 6, 0:D], ACT.Copy).then_inc(s["act_weights"], 1)
            act.activation(gateT[:], PS[:, 7, 0:NH * E].rearrange("p (h e) -> p h e", h=NH), ACT.Copy).then_inc(s["act_weights"], 1)
            act.wait_ge(s["pe_post"], 4)
            act.activation(xqT[:], bank16(5)[:, 0:NH * T].rearrange("p (h t) -> p h t", h=NH), ACT.Copy).then_inc(s["act_post"], 1)
            act.wait_ge(s["pe_post"], 6)
            act.activation(xT16[:, 0], PS[:, 0:2, 0:T], ACT.Copy).then_inc(s["act_post"], 1)
            act.activation(xT[:], PS[:, 0:2, 0:T], ACT.Copy).then_inc(s["act_post"], 1)
            act.wait_ge(s["dve_post"], 6)
            act.activation(r[1][:], r[2][:], ACT.Exp).then_inc(s["act_post"], 1)
            act.wait_ge(s["sp_ready"], 1)
            act.activation(r[4][:], r[5][:], ACT.Sqrt).then_inc(s["act_post"], 1)
            act.activation(tg[:, 1:2], gx[:, 1:2], ACT.Tanh).then_inc(s["act_post"], 1)

            def weights_hi(q, n):
                after(act, "wt_ready", n)
                act.activation(w13T[q][:, 0], PS[:, 4:6, 0:2 * I], ACT.Copy, scale=FS)
                act.activation(w2T[q][:, 0], PS[0:IH, 3, :], ACT.Copy, scale=FS).then_inc(s["wh_done"], 1)

            def expert(e, q, prepare):
                def tanh(t):
                    after(act, "gu_ready", e * TT + t + 1)
                    if t == 0:
                        after(act, "h_done", e * TT)
                    act.activation(th[:, t, :], PS[0:TP, g_bank[t], 0:I], ACT.Tanh, scale=0.5 / FS).then_inc(s["tanh_done"], 1)

                def h_hi(p):
                    after(act, "ht_ready", e * 2 + p + 1)
                    after(act, "y_ready", e * 2)
                    act.activation(hT[:, 0, p, :], PS[0:IH, h_bank[p], 0:4 * TP], ACT.Copy).then_inc(s["hh_done"], 1)

                for t in range(TT):
                    tanh(t)
                h_hi(0)
                h_hi(1)
                if prepare:
                    weights_hi(1 - q, e + 2)

            weights_hi(0, 1)
            with act.Fori(0, E // 2) as it:
                for q in range(2):
                    expert(it * 2 + q, q, True)
            expert(E, 0, False)

        @block.vector
        def _(dve):
            d = Steps(dve, s["dve_step"])

            def quantise(src, n, am_, s_, out16, k=d):
                k.settle()
                k.did(dve.tensor_reduce(am_[:, 0:n], src[:], AX.X, ALU.max, apply_absolute_value=True))
                k.settle()
                k.did(dve.tensor_scalar(s_[:], am_[:, 0:n], 1.0 / 127, 1e-8, ALU.mult, ALU.max))
                k.settle()
                k.did(dve.reciprocal(am_[:, 0:n], s_[:]))
                k.settle()
                for r_ in range(n):
                    k.did(dve.tensor_scalar(src[:, r_, :], src[:, r_, :], am_[:, r_:r_ + 1], 127.0, ALU.mult, ALU.min))
                k.settle()
                k.did(dve.tensor_scalar(src[:], src[:], -127.0, MAGIC, ALU.max, ALU.add))
                k.settle()
                return dve.tensor_scalar(out16[:], src[:], MAGIC, None, ALU.subtract)

            def context_lo(n, u, bank=None):
                c, hf = divmod(u, 2)
                after(dve, "th_done", n * 6 + u + 1)
                dve.tensor_tensor(cT[:, 1, hf, c * CW:(c + 1) * CW], PS[:, t_bank[u] if bank is None else bank, 0:CW],
                                  cT[:, 0, hf, c * CW:(c + 1) * CW], ALU.subtract).then_inc(s["tl_done"], 1)

            def layernorm(src, dst, nth):
                d.settle()
                for t in range(TT):
                    d.did(dve.bn_stats(st[:, t, :], src[:, t, :]))
                d.settle()
                for t in range(TT):
                    d.did(dve.bn_aggr(mv[:, t, :], st[:, t, :]))
                d.settle()
                dve.tensor_scalar(var[:], mv[:, :, 1], EPS, None, ALU.add).then_inc(s["var_ready"], 1)
                dve.wait_ge(s["rstd_ready"], nth)
                for t in range(TT):
                    last = dve.tensor_scalar(dst[:, t, :], src[:, t, :], mv[:, t, 0:1], rstd[:, t:t + 1], ALU.subtract, ALU.mult)
                return last

            dve.wait_ge(s["x_loaded"], 16)
            d.did(layernorm(x_in, xn, 1))
            quantise(xn, TT, am[0:TP], sx, xq16).then_inc(s["xq_ready"], 1)
            dve.wait_ge(s["consts"], NCONST)
            for t in range(TT):
                last = dve.tensor_scalar(diag[0:TP, t, 0:TP], ident[0:TP, 0:TP], sx[:, t:t + 1], None, ALU.mult)
            last.then_inc(s["sx_diag"], 1)
            dve.wait_ge(s["act_pre"], 1)
            dve.scalar_tensor_tensor(wkvT[:, 1], PS[:, 0:2, :], WS, wkvT[:, 0], ALU.mult, ALU.subtract).then_inc(s["dve_pre"], 1)
            dve.wait_ge(s["wq_loaded"], 16)
            quantise(wq_in, NH, am, swq, wq16).then_inc(s["wqq_ready"], 1)
            for u in range(6):
                context_lo(0, u, t0_bank[u])
            dve.wait_ge(s["small_loaded"], NSMALL)
            dve.wait_ge(s["act_pre"], 5)
            dve.wait_ge(s["pe_pre"], 5)
            for oh in range(NH):
                d.did(dve.scalar_tensor_tensor(qT[:, oh, :], PS[:, 2 + oh, 0:T], swq[:, oh:oh + 1], sx_row[:], ALU.mult, ALU.mult))
            d.settle()
            for g in range(G):
                own = slice(64 * (g % 2), 64 * (g % 2) + 64)
                for k in range(2):
                    d.did(dve.tensor_scalar(qd[64 * k:64 * k + 64, g // 2, g % 2, :], qT[own, g // 2, :], bq_c[own, g // 2:g // 2 + 1], None, ALU.add))
            d.settle()
            q4 = q16.rearrange("p (a b) k t -> p a b k t", a=2)
            d.did(dve.tensor_copy(q4[:, :, :, 0], qd[:]))
            d.settle()
            dve.tensor_tensor(q4[:, :, :, 1], qd[:], q4[:, :, :, 0], ALU.subtract).then_inc(s["qs_ready"], 1)
            pre_steps = d.n

            def keys_lo(n, oh, c, bank=None):
                after(dve, f"kh{oh}_done", n * 6 + 2 * c + 2)
                for k in range(2):
                    own, other = slice(64 * k, 64 * k + 64), slice(64 - 64 * k, 128 - 64 * k)
                    cols = slice(c * CW, (c + 1) * CW)
                    last = dve.scalar_tensor_tensor(KS[other, 2 * oh + k, cols], PS[own, bank or k_bank[oh][c], 0:CW], bk_c[own, oh:oh + 1],
                                                    KS[own, 2 * oh + k, cols], ALU.add, ALU.subtract)
                last.then_inc(s[f"kl{oh}_done"], 1)

            def dve_sequence(b, prepare):
                n = b + 1
                step = Steps(dve, s["dve_step"], b * SEQ_STEPS + pre_steps)

                def row_max(i):
                    for k, c in enumerate(order):
                        after(dve, "sc_ready", b * SCN + i * CH + k + 1)
                        step.did(dve.tensor_reduce(mx[:, i, c:c + 1], PS[0:TP, 3 * (i % 2) + c, 0:CW], AX.X, ALU.max))
                    step.settle()
                    step.did(dve.scalar_tensor_tensor(mx[:, i, 3:4], mx[:, i, 0:1], mx[:, i, 1:2], mx[:, i, 2:3], ALU.max, ALU.max))
                    step.settle()
                    dve.tensor_scalar(nmx[:, i:i + 1], mx[:, i, 3:4], -SCORE, None, ALU.mult).then_inc(s["max_done"], 1)

                def pt_evac(i):
                    after(dve, "tr_ready", b * NPAIR + i + 1)
                    dve.tensor_copy(PT[:, i, 8 * TP:KT * TP], PS[0:KP, 3 * (i % 2) + 2, 0:4 * TP]).then_inc(s["pt_dve"], 1)

                def o_evac(gh):
                    after(dve, "pv_ready", b * 2 + gh + 1)
                    step.did(dve.tensor_scalar(oe[:, gh], PS[:, o_bank[gh], 0:S], par[:, 0:1], None, ALU.mult))
                    step.settle()
                    dve.scalar_tensor_tensor(OT[:, gh, bass.ds(b * S, S)], PS[:, o_bank[gh], S:2 * S], par[:, 1:2], oe[:, gh],
                                             ALU.mult, ALU.add).then_inc(s["o_done"], 1)

                after(dve, "pv_ready", b * 2)
                after(dve, "exp_done", b * NPAIR)

                def next_context(*units):
                    if prepare:
                        for u in units:
                            context_lo(n, u)

                def next_keys(c):
                    if prepare:
                        keys_lo(n, 0, c)

                row_max(0)
                keys_lo(b, 1, 0)
                row_max(1)
                pt_evac(0)
                keys_lo(b, 1, 1)
                row_max(2)
                pt_evac(1)
                keys_lo(b, 1, 2)
                row_max(3)
                pt_evac(2)
                next_context(0, 1)
                row_max(4)
                pt_evac(3)
                next_keys(0)
                row_max(5)
                next_context(2)
                pt_evac(4)
                next_context(3)
                pt_evac(5)
                row_max(6)
                next_context(4, 5)
                if not prepare:
                    dve.wait_ge(s["wp_loaded"], 16)
                    quantise(wp_in, NH, am, swp, wp16, step).then_inc(s["wpq_ready"], 1)
                row_max(7)
                next_keys(1)
                pt_evac(6)
                pt_evac(7)
                next_keys(2)
                o_evac(0)
                o_evac(1)
                assert step.n == SEQ_STEPS + (0 if prepare else WP_STEPS)

            for c in range(CH):
                keys_lo(0, 0, c, bank=k0_bank[c])
            with dve.Fori(0, B - 1) as b:
                dve_sequence(b, True)
            dve_sequence(B - 1, False)

            d.base = B * SEQ_STEPS + WP_STEPS
            pn = [0]

            def post(ins):
                pn[0] += 1
                ins.then_inc(s["dve_post"], 1)

            for k in range(NH):
                last = dve.tensor_scalar(diag[:, k, :], ident[:], swp[:, k:k + 1], None, ALU.mult)
            last.then_inc(s["sp_diag"], 1)
            dve.wait_ge(s["pe_post"], 2)
            rd_v = rd[:].rearrange("p t (i a) -> p t a i", a=2)
            for t in range(TT):
                d.did(dve.tensor_scalar(rd_v[:, t], PS[0:TP, 2, t * H:(t + 1) * H].rearrange("p (a i) -> p a i", a=2), WS, None, ALU.mult))
            d.settle()
            d.did(dve.reciprocal(rd[:], rd[:]))
            d.settle()
            dve.wait_ge(s["pe_post"], 3)
            for t in range(TT):
                o_v = xn[:, t, :].rearrange("p (h j) -> p h j", h=H)
                d.did(dve.tensor_tensor(o_v, PS[0:TP, 3 + t // 2, (t % 2) * D:(t % 2 + 1) * D].rearrange("p (h j) -> p h j", h=H),
                                        rd[:, t, :].unsqueeze(2).to_broadcast([TP, H, DH]), ALU.mult))
            d.settle()
            for t in range(TT):
                d.did(dve.tensor_tensor(xn[:, t, :], xn[:, t, :], bv_r[:], ALU.add))
            post(quantise(xn, TT, am[0:TP], so, xq16))
            dve.wait_ge(s["act_weights"], 3)
            dve.wait_ge(s["pe_post"], 5)
            for t in range(TT):
                d.did(dve.scalar_tensor_tensor(xn[:, t, :], PS[0:TP, 6 + t // 2, (t % 2) * D:(t % 2 + 1) * D], so[:, t:t + 1],
                                               sp_row[:], ALU.mult, ALU.mult))
            d.settle()
            for t in range(TT):
                d.did(dve.tensor_tensor(xn[:, t, :], xn[:, t, :], bp_r[:], ALU.add))
            d.settle()
            for t in range(TT):
                d.did(dve.scalar_tensor_tensor(x1[:, t, :], xn[:, t, :], tg[:, 0:1], x_in[:, t, :], ALU.mult, ALU.add))
            post(layernorm(x1, xn, 2))
            dve.wait_ge(s["act_post"], 4)
            post(dve.tensor_tensor(xT16[:, 1], xT[:], xT16[:, 0], ALU.subtract))
            logit, e_, z, z2, acc, a, b_, c_ = (r[0], r[1], r[2], r[3], r[4], r[5], r[6], r[7])
            dve.wait_ge(s["pe_post"], 7)
            post(dve.tensor_copy(logit[:], PS[0:TP, 2, 0:TT * E].rearrange("p (t e) -> p t e", t=TT)))
            dve.wait_ge(s["dve_post"], 4)
            post(dve.tensor_scalar(z[:], logit[:], -1.0, None, ALU.mult))
            dve.wait_ge(s["dve_post"], 5)
            post(dve.tensor_tensor(z[:], z[:], logit[:], ALU.min))
            dve.wait_ge(s["act_post"], 5)
            def one(ins):
                d.did(ins)
                d.settle()
            one(dve.tensor_scalar(a[:], e_[:], 2.0, None, ALU.add))
            one(dve.reciprocal(a[:], a[:]))
            one(dve.tensor_tensor(z[:], e_[:], a[:], ALU.mult))
            one(dve.tensor_tensor(z2[:], z[:], z[:], ALU.mult))
            one(dve.tensor_scalar(acc[:], z2[:], 2.0 / 17, 2.0 / 15, ALU.mult, ALU.add))
            for k in (13, 11, 9, 7, 5, 3, 1):
                one(dve.tensor_tensor(acc[:], acc[:], z2[:], ALU.mult))
                one(dve.tensor_scalar(acc[:], acc[:], 2.0 / k, None, ALU.add))
            one(dve.tensor_tensor(acc[:], acc[:], z[:], ALU.mult))
            dve.scalar_tensor_tensor(a[:], logit[:], 0.0, acc[:], ALU.max, ALU.add).then_inc(s["sp_ready"], 1)
            dve.wait_ge(s["act_post"], 6)
            sc, bias = acc, z2
            one(dve.tensor_tensor(bias[:], sc[:], gb_r[:].unsqueeze(1).to_broadcast([TP, TT, E]), ALU.add))
            for k, oh in enumerate((e_, z)):
                one(dve.tensor_reduce(rs[0][:], bias[:], AX.X, ALU.max))
                one(dve.tensor_tensor(a[:], bias[:], rs[0][:].unsqueeze(2).to_broadcast([TP, TT, E]), ALU.is_ge))
                one(dve.tensor_tensor(a[:], a[:], rank[:], ALU.mult))
                one(dve.tensor_reduce(rs[0][:], a[:], AX.X, ALU.max))
                one(dve.tensor_tensor(oh[:], a[:], rs[0][:].unsqueeze(2).to_broadcast([TP, TT, E]), ALU.is_equal))
                one(dve.tensor_tensor(b_[:], sc[:], oh[:], ALU.mult))
                one(dve.tensor_reduce(rs[1 + k][:], b_[:], AX.X, ALU.add))
                if k == 0:
                    one(dve.scalar_tensor_tensor(bias[:], oh[:], -3e38, bias[:], ALU.mult, ALU.add))
            d.did(dve.tensor_tensor(c_[:], e_[:], z[:], ALU.add))
            one(dve.tensor_tensor(rs[3][:], rs[1][:], rs[2][:], ALU.add))
            post(dve.tensor_copy(sel16[:], c_[:]))
            one(dve.reciprocal(rs[3][:], rs[3][:]))
            for k, oh in enumerate((e_, z)):
                one(dve.tensor_tensor(rs[1 + k][:], rs[1 + k][:], rs[3][:], ALU.mult))
                one(dve.tensor_tensor(oh[:], oh[:], rs[1 + k][:].unsqueeze(2).to_broadcast([TP, TT, E]), ALU.mult))
            one(dve.tensor_tensor(a[:], e_[:], z[:], ALU.add))
            dve.wait_ge(s["pe_post"], 8)
            one(dve.tensor_scalar(b_[:], PS[0:TP, 7, 0:TT * E].rearrange("p (t e) -> p t e", t=TT), CAP - 0.5, 0.5 / FS, ALU.is_lt, ALU.mult))
            d.did(dve.tensor_tensor(WT[:, 0:E * TT].rearrange("p (e t) -> p t e", t=TT), a[:], b_[:], ALU.mult))
            d.settle()
            dve.wait_ge(s["act_post"], 7)
            one(dve.tensor_scalar(tgf[:], tg[:, 1:2], 1.0 / (FS * FS), None, ALU.mult))
            post_steps = d.n

            def weights_lo(q, n):
                after(dve, "wh_done", n)
                dve.scalar_tensor_tensor(w13T[q][:, 1], PS[:, 4:6, 0:2 * I], FS, w13T[q][:, 0], ALU.mult, ALU.subtract).then_inc(s["w13l_done"], 1)
                dve.scalar_tensor_tensor(w2T[q][:, 1], PS[0:IH, 3, :], FS, w2T[q][:, 0], ALU.mult, ALU.subtract).then_inc(s["wl_done"], 1)

            def expert(e, q, prepare):
                own = Steps(dve, s["dve_step"], e * (TT + 1) + (d.base + post_steps))
                own.did(dve.tensor_copy(wcur[:, q, :], WT[:, bass.ds(e * TT, TT)]))

                def hidden(t):
                    after(dve, "tanh_done", e * TT + t + 1)
                    own.did(dve.scalar_tensor_tensor(hg[:, t, :], th[:, t, :], 1.0, PS[0:TP, g_bank[t], 0:I], ALU.add, ALU.mult))
                    own.settle()
                    dve.scalar_tensor_tensor(hn[:, t, :], PS[0:TP, g_bank[t], I:2 * I], wcur[:, q, t:t + 1], hg[:, t, :],
                                             ALU.mult, ALU.mult).then_inc(s["h_done"], 1)

                def h_lo(p):
                    after(dve, "hh_done", e * 2 + p + 1)
                    dve.tensor_tensor(hT[:, 1, p, :], PS[0:IH, h_bank[p], 0:4 * TP], hT[:, 0, p, :], ALU.subtract).then_inc(s["hl_done"], 1)

                after(dve, "ht_ready", e * 2)
                for t in range(TT):
                    hidden(t)
                h_lo(0)
                h_lo(1)
                if prepare:
                    weights_lo(1 - q, e + 2)
                assert own.n == TT + 1

            weights_lo(0, 1)
            with dve.Fori(0, E // 2) as it:
                for q in range(2):
                    expert(it * 2 + q, q, True)
            expert(E, 0, False)
            after(dve, "y_ready", 2 * (E + 1))
            for t in range(TT):
                last = dve.scalar_tensor_tensor(y_out[:, t, :], PS[0:TP, t // 2, (t % 2) * D:(t % 2 + 1) * D], tgf[:, 0:1], x1[:, t, :],
                                                ALU.mult, ALU.add)
            last.then_inc(s["y_final"], 1)

        @block.tensor
        def _(pe):
            mm, tp = pe.matmul, pe.transpose

            def split3(out_, w, x_, first=True, last=True, halves=2):
                todo = [(a, b, h) for a, b in SPLIT for h in range(halves)]
                for k, (a, b, h) in enumerate(todo):
                    ins = mm(out_, w(a, h), x_(b, h), start=first and k == 0, stop=last and k == len(todo) - 1)
                return ins

            pe.wait_ge(s["consts"], NCONST)
            pe.wait_ge(s["wkv_loaded"], 16)
            for h in range(NH):
                for k in range(2 * NH):
                    last = tp(PS[:, h, k * 128:(k + 1) * 128], wkv_in[:, k, h * 128:(h + 1) * 128], ident[:])
            last.then_inc(s["pe_pre"], 1)

            def context(n, u, b=None):
                c, hf = divmod(u, 2)
                if hf == 0:
                    pe.wait_ge(ctx_in[c], n * 16 + 16)
                if b is None:
                    if u == 5:
                        pe.wait_ge(s["dve_pre"], 1)
                elif u == 5:
                    after(pe, "tl_done", n * 6 + 4)
                elif u == 0:
                    after(pe, "kl1_done", b * 3 + 3)
                else:
                    after(pe, "v_act", b * 6 + u + 2)
                for j in range(4):
                    last = tp(PS[:, (t0_bank if b is None else t_bank)[u], j * KP:(j + 1) * KP], c_in[:, 4 * c + j, hf * 128:(hf + 1) * 128], ident[0:KP, 0:KP])
                last.then_inc(s["t_ready"], 1)

            def keys(n, oh, c, bank=None):
                if oh == 0:
                    after(pe, "tl_done", n * 6 + ((2, 5, 6) if bank is None else (3, 4, 6))[c])
                elif c == 0:
                    after(pe, "o_done", n * 2)
                else:
                    after(pe, "v_act", n * 6 + c)
                split3(PS[:, bank or k_bank[oh][c], 0:CW], lambda a, h: wkvT[:, a, h, oh * 128:(oh + 1) * 128],
                       lambda a, h: cT[:, a, h, c * CW:(c + 1) * CW]).then_inc(s[f"k{oh}_ready"], 1)

            def pe_sequence(b, prepare):
                n = b + 1

                def scores(i):
                    if i == 0:
                        after(pe, "kl0_done", b * 3 + 3)
                        after(pe, "qc0_done", b + 1)
                    elif i == 4:
                        after(pe, "kl1_done", b * 3 + 3)
                        after(pe, "qc1_done", b + 1)
                    g, j = divmod(i, 2)
                    for c in order:
                        if c != 1:
                            after(pe, "pt_dve" if c == 2 else "pt_act", b * NPAIR + max(i - 1, 0))
                        for k in range(2):
                            last = mm(PS[0:TP, 3 * (i % 2) + c, 0:CW], QC[:, (g * 2 + k) * 4 * S + j * TP:(g * 2 + k) * 4 * S + (j + 1) * TP],
                                      KS[:, g, c * CW:(c + 1) * CW], start=k == 0, stop=k == 1)
                        last.then_inc(s["sc_ready"], 1)

                def values(v):
                    if v == 0:
                        after(pe, "o_done", b * 2)
                    elif v < 3:
                        after(pe, "kl1_done", b * 3 + v)
                    elif v == 3:
                        if prepare:
                            after(pe, "tl_done", n * 6 + 1)
                        else:
                            after(pe, "kl1_done", b * 3 + 3)
                    elif not prepare:
                        after(pe, "v_act", b * 6 + v - 1)
                    elif v == 4:
                        after(pe, "kl0_done", n * 3 + 1)
                    else:
                        after(pe, "tl_done", n * 6 + 3)
                    for k in range(2):
                        t = 2 * v + k
                        last = split3(PS[0:KP, v_bank[v], k * D:(k + 1) * D], lambda a, h: cT[:, a, h, t * KP:(t + 1) * KP],
                                      lambda a, h: wkvT[:, a, h, D:2 * D])
                    last.then_inc(s["v_ready"], 1)

                def turn(i):
                    after(pe, "exp_done", b * NPAIR + i + 1)
                    for t in range(KT):
                        last = tp(PS[0:KP, 3 * (i % 2) + t // 4, (t % 4) * TP:(t % 4 + 1) * TP], P[:, i % 2, t * KP:(t + 1) * KP],
                                  ident[0:TP, 0:TP])
                    last.then_inc(s["tr_ready"], 1)

                def outputs(gh, t0, t1):
                    if t0 == 0:
                        after(pe, "pt_act", b * NPAIR + 4 * gh + 4)
                        after(pe, "pt_dve", b * NPAIR + 4 * gh + 4)
                        if gh == 0:
                            after(pe, "v_act", b * 6 + 6)
                        if prepare:
                            after(pe, "kl0_done", n * 3 + 2 + gh)
                    for t in range(t0, t1):
                        for j in range(4):
                            i = 4 * gh + j
                            last = mm(PS[32 * j:32 * j + 32, o_bank[gh], 0:TP], V[:, t, i * 32:(i + 1) * 32],
                                      PT[:, i, t * TP:(t + 1) * TP], start=t == 0, stop=t == KT - 1,
                                      tile_position=(0, 32 * j))
                    if t1 == KT:
                        last.then_inc(s["pv_ready"], 1)

                def next_context(*units):
                    if prepare:
                        for u in units:
                            context(n, u, b)

                def next_keys(*chunks):
                    if prepare:
                        for c in chunks:
                            keys(n, 0, c)

                scores(0)
                keys(b, 1, 0)
                values(0)
                scores(1)
                keys(b, 1, 1)
                turn(0)
                values(1)
                scores(2)
                keys(b, 1, 2)
                turn(1)
                values(2)
                scores(3)
                next_context(0)
                turn(2)
                next_context(1)
                scores(4)
                next_keys(0)
                turn(3)
                values(3)
                scores(5)
                values(4)
                next_context(2)
                turn(4)
                next_context(3)
                values(5)
                turn(5)
                scores(6)
                next_context(4, 5)
                scores(7)
                next_keys(1, 2)
                turn(6)
                outputs(0, 0, 3)
                turn(7)
                outputs(0, 3, KT)
                outputs(1, 0, KT)

            for u in range(5):
                context(0, u)
            pe.wait_ge(s["xq_ready"], 1)
            for h in range(NH):
                for t in range(TT):
                    last = tp(bank16(7)[:, h * T + t * TP:h * T + (t + 1) * TP], xq16[:, t, h * 128:(h + 1) * 128], ident16[0:TP, 0:TP])
            last.then_inc(s["pe_pre"], 1)
            pe.wait_ge(s["sx_diag"], 1)
            pe.wait_ge(s["dve_pre"], 1)
            for t in range(TT):
                last = mm(PS[:, 1, t * TP:(t + 1) * TP], ones[0:TP, :], diag[0:TP, t, 0:TP], start=True, stop=True)
            last.then_inc(s["pe_pre"], 1)
            context(0, 5)
            pe.wait_ge(s["wqq_ready"], 1)
            pe.wait_ge(s["act_pre"], 4)
            for h in range(NH):
                for k in range(NH):
                    last = tp(bank16(7)[:, h * D + k * 128:h * D + (k + 1) * 128], wq16[:, k, h * 128:(h + 1) * 128], ident16[:])
            last.then_inc(s["pe_pre"], 1)
            pe.wait_ge(s["act_pre"], 6)
            after(pe, "tl_done", 2)
            for k in range(NH):
                for h in range(NH):
                    last = mm(PS[:, 2 + k, 0:T], wqT[:, h, k * 128:(k + 1) * 128], xqT[:, h, :], start=h == 0, stop=h == NH - 1)
            last.then_inc(s["pe_pre"], 1)
            for c in range(CH):
                keys(0, 0, c, bank=k0_bank[c])
            with pe.Fori(0, B - 1) as b:
                pe_sequence(b, True)
            pe_sequence(B - 1, False)

            after(pe, "o_done", 2 * B)
            after(pe, "pt_dve", NPAIR * B)
            pe.wait_ge(s["wpq_ready"], 1)
            for h in range(NH):
                for k in range(NH):
                    last = tp(bank16(5)[:, h * D + k * 128:h * D + (k + 1) * 128], wp16[:, k, h * 128:(h + 1) * 128], ident16[:])
            last.then_inc(s["pe_weights"], 1)
            after(pe, "den_saved", B)
            after(pe, "o_done", 2 * B)
            after(pe, "pt_act", NPAIR * B)
            after(pe, "pt_dve", NPAIR * B)
            for k in range(B):
                last = tp(PS[0:NPAIR, k // 4, (k % 4) * TP:(k % 4 + 1) * TP], den_all[:, k * NPAIR:(k + 1) * NPAIR], ident[0:TP, 0:TP])
            last.then_inc(s["pe_post"], 1)
            pe.wait_ge(s["act_post"], 1)
            dT_v = dT[:].rearrange("p (a k) -> p a k", a=2)
            for t in range(TT):
                for a in range(2):
                    last = tp(PS[0:TP, 2, t * H + a * NPAIR:t * H + (a + 1) * NPAIR], dT_v[:, a, t * TP:(t + 1) * TP], ident[0:NPAIR, 0:NPAIR])
            last.then_inc(s["pe_post"], 1)
            for t in range(TT):
                for g in range(2):
                    last = tp(PS[0:TP, 3 + t // 2, (t % 2) * D + g * 128:(t % 2) * D + (g + 1) * 128], OT[:, g, t * TP:(t + 1) * TP], ident[:])
            last.then_inc(s["pe_post"], 1)
            pe.wait_ge(s["small_loaded"], NSMALL)
            for h in range(NH):
                tp(PS[:, 7, h * E:(h + 1) * E], gate_in[:, h * 128:(h + 1) * 128], ident[0:E, 0:E])
            pe.wait_ge(s["sp_diag"], 1)
            for k in range(NH):
                last = mm(PS[0:TP, 6, k * 128:(k + 1) * 128], ones[:, 0:TP], diag[:, k, :], start=True, stop=True)
            last.then_inc(s["pe_weights"], 1)
            pe.wait_ge(s["act_weights"], 3)
            pe.wait_ge(s["dve_post"], 1)
            for h in range(NH):
                for t in range(TT):
                    last = tp(bank16(5)[:, h * T + t * TP:h * T + (t + 1) * TP], xq16[:, t, h * 128:(h + 1) * 128], ident16[0:TP, 0:TP])
            last.then_inc(s["pe_post"], 1)
            pe.wait_ge(s["act_post"], 2)
            for t in range(TT):
                for h in range(NH):
                    last = mm(PS[0:TP, 6 + t // 2, (t % 2) * D:(t % 2 + 1) * D], xqT[:, h, t * TP:(t + 1) * TP], wpT[:, h, :], start=h == 0, stop=h == NH - 1)
            last.then_inc(s["pe_post"], 1)
            pe.wait_ge(s["dve_post"], 2)
            for h in range(NH):
                for t in range(TT):
                    last = tp(PS[:, h, t * TP:(t + 1) * TP], xn[:, t, h * 128:(h + 1) * 128], ident[0:TP, 0:TP])
            last.then_inc(s["pe_post"], 1)

            def weights(q, n):
                pe.wait_ge(w_in[q], ((n + 1) // 2) * 48 if isinstance(n, int) else n)
                for k in range(2):
                    for h in range(NH):
                        tp(PS[0:IH, 3, k * D + h * 128:k * D + (h + 1) * 128], w2_in[q][:, h, k * IH:(k + 1) * IH], ident[:])
                for h in range(NH):
                    for k in range(4):
                        last = tp(PS[:, 4 + h, k * IH:(k + 1) * IH], w13_in[q][:, k, h * 128:(h + 1) * 128], ident[0:IH, 0:IH])
                last.then_inc(s["wt_ready"], 1)

            pe.wait_ge(s["act_post"], 4)
            for t in range(TT):
                for h in range(NH):
                    last = mm(PS[0:TP, 2, t * E:(t + 1) * E], xT[:, h, t * TP:(t + 1) * TP], gateT[:, h, :], start=h == 0, stop=h == NH - 1)
            last.then_inc(s["pe_post"], 1)
            weights(0, 1)
            for k in range(2):
                mm(PS[0:TP, k, :], zero16[:, 0:TP], zero16[:], start=True, stop=False, skip_group_check=True)
            pe.wait_ge(s["dve_post"], 7)
            for t in range(TT):
                for k in range(t + 1):
                    last = mm(PS[0:TP, 7, t * E:(t + 1) * E], (before16 if k == t else ones16)[:], sel16[:, k, :],
                              start=k == 0, stop=k == t)
            last.then_inc(s["pe_post"], 1)
            pe.wait_ge(s["dve_post"], 7)

            def expert(e, q, prepare, final=False):
                def gate_up(t):
                    if t == 0:
                        after(pe, "hl_done", e * 2)
                        after(pe, "h_done", e * TT)
                    elif t == 3:
                        after(pe, "h_done", e * TT + 1)
                    split3(PS[0:TP, g_bank[t], 0:2 * I], lambda a, h: xT16[:, a, h, t * TP:(t + 1) * TP],
                           lambda a, h: w13T[q][:, a, h, :]).then_inc(s["gu_ready"], 1)

                def turn_h(p):
                    after(pe, "h_done", e * TT + 2 * p + 2)
                    for k in range(2):
                        for t in range(2):
                            last = tp(PS[0:IH, h_bank[p], (k * 2 + t) * TP:(k * 2 + t + 1) * TP], hn[:, 2 * p + t, k * IH:(k + 1) * IH], ident[0:TP, 0:TP])
                    last.then_inc(s["ht_ready"], 1)

                def down(p):
                    after(pe, "hl_done", e * 2 + p + 1)
                    for t in range(2):
                        todo = [(a, b, k) for a, b in SPLIT for k in range(2)]
                        for n, (a, b, k) in enumerate(todo):
                            last = mm(PS[0:TP, p, t * D:(t + 1) * D], hT[:, a, p, (k * 2 + t) * TP:(k * 2 + t + 1) * TP],
                                      w2T[q][:, b, k * D:(k + 1) * D], start=False, stop=final and n == len(todo) - 1,
                                      skip_group_check=True)
                    last.then_inc(s["y_ready"], 1)

                after(pe, "w13l_done", e + 1)
                gate_up(0)
                after(pe, "wl_done", e + 1)
                for t in range(1, TT):
                    gate_up(t)
                turn_h(0)
                if prepare is not None:
                    weights(1 - q, prepare)
                turn_h(1)
                down(0)
                down(1)

            pe.wait_ge(s["dve_post"], 3)

            with pe.Fori(0, E // 2) as it:
                expert(it * 2, 0, it * 48 + 48)
                expert(it * 2 + 1, 1, it * 48 + 96)
            expert(E, 0, None, final=True)


_INS = ["x", "ctx_2048", "g_xattn", "g_ffn", "L0_xattn_wq", "L0_xattn_bq", "L0_xattn_wkv", "L0_xattn_bkv",
        "L0_xattn_wp", "L0_xattn_bp", "L0_ffn_gate_w", "L0_ffn_gate_b", "L0_ffn_W1", "L0_ffn_W3", "L0_ffn_W2",
        "L0_ffn_Ws1", "L0_ffn_Ws3", "L0_ffn_Ws2"]


def kernel(**inputs):
    import numpy as np
    import concourse.bacc as bacc
    from concourse.bass_utils import run_bass_kernel_spmd

    nc = bacc.Bacc("TRN2", target_bir_lowering=False, num_devices=1)
    arrays, args = {}, []
    for name in _INS:
        a = np.ascontiguousarray(inputs[name])
        arrays[name] = a
        args.append(nc.dram_tensor(name, a.shape, mybir.dt.from_np(a.dtype), kind="ExternalInput").ap())
    args.append(nc.dram_tensor("y", (B, S, D), F32, kind="ExternalOutput").ap())
    program(nc, *args)
    return run_bass_kernel_spmd(nc, [arrays], core_ids=[0]).results[0]["y"]
```

```python
import concourse.bass as bass
from concourse import mybir
from contextlib import ExitStack

F32 = mybir.dt.float32
F16 = mybir.dt.float16
ALU = mybir.AluOpType
ACT = mybir.ActivationFunctionType
AX = mybir.AxisListType

B, S, D = 8, 56, 256
M = 1500
H, DH = 16, 16
E, I = 16, 176
CAP = 128
T = B * S
TP, TT = 112, 4
NH = D // 128
KP, KT = 125, 12
CH = 3
CW = M // CH
NPAIR = H // 2
PW = 2 * DH
QW = NPAIR * 2 * S
STACKED = 16 * 4 * CH
IH = I // 2
WS = 64.0
FS = 16.0
SCORE = DH ** -0.5 / WS
MAGIC = 1.5 * 2.0 ** 23
EPS = 1e-5
W_COL = 256
NCONST = 18
NSMALL = 10 * 16
SEQ_STEPS = 4 * NPAIR + 2
WP_STEPS = 4 + NH
SCN = NPAIR * CH
SPLIT = ((0, 0), (0, 1), (1, 0))


class Steps:

    def __init__(self, eng, sem, base=0):
        self.eng, self.sem, self.base, self.n = eng, sem, base, 0

    def did(self, ins):
        ins.then_inc(self.sem, 1)
        self.n += 1

    def settle(self):
        self.eng.wait_ge(self.sem, self.base + self.n)


def program(nc, x, ctx, g_xattn, g_ffn, wq, bq, wkv, bkv, wp, bp, gate_w, gate_b, W1, W3, W2, Ws1, Ws3, Ws2, out):
    stack = ExitStack()
    with stack:
        def sb(name, shape, dt=F32):
            return stack.enter_context(nc.sbuf_tensor(name, shape, dt))

        def sem(name):
            return stack.enter_context(nc.semaphore(name))

        ident = sb("ident", [128, 128])
        ident16 = sb("ident16", [128, 128], F16)
        ones = sb("ones", [128, 128])
        ones16 = sb("ones16", [TP, TP], F16)
        before16 = sb("before16", [TP, TP], F16)
        hm2 = sb("hm2", [128, 2, 4])
        hmask = sb("hmask", [128, 4])
        par = sb("par", [128, 2])
        rank = sb("rank", [TP, TT, E])
        x_in = sb("x_in", [TP, TT, D])
        wq_in = sb("wq_in", [128, NH, D])
        wp_in = sb("wp_in", [128, NH, D])
        wkv_in = sb("wkv_in", [128, 2 * NH, D])
        gate_in = sb("gate_in", [E, D])
        bq_c = sb("bq_c", [128, NH])
        bk_c = sb("bk_c", [128, NH])
        bv_r = sb("bv_r", [TP, D])
        bp_r = sb("bp_r", [TP, D])
        gb_r = sb("gb_r", [TP, E])
        gx = sb("gx", [TP, 2])
        tg = sb("tg", [TP, 2])
        tgf = sb("tgf", [TP, 1])
        st = sb("st", [TP, TT, 6])
        mv = sb("mv", [TP, TT, 2])
        var = sb("var", [TP, TT])
        mhalf = sb("mhalf", [TP, TT])
        rstd = sb("rstd", [TP, TT])
        am = sb("am", [128, TT])
        sx = sb("sx", [TP, TT])
        swq = sb("swq", [128, NH])
        swp = sb("swp", [128, NH])
        so = sb("so", [TP, TT])
        xn = sb("xn", [TP, TT, D])
        xq16 = sb("xq16", [TP, TT, D], F16)
        wq16 = sb("wq16", [128, NH, D], F16)
        wp16 = sb("wp16", [128, NH, D], F16)
        wqT = sb("wqT", [128, NH, D], F16)
        wpT = sb("wpT", [128, NH, D], F16)
        xqT = sb("xqT", [128, NH, T], F16)
        diag = sb("diag", [128, TT, 128])
        sx_row = sb("sx_row", [128, T])
        sp_row = sb("sp_row", [TP, D])
        qT = sb("qT", [128, NH, T])
        LATE = 2 * (NH * T + 2 * 2 * NH * I + 2 * 2 * D + 2 * TT * TP) + 2 * TT * D + 2 * TT * CAP + 2 * NH * CAP + 2 * T + 2 * D + 4 * CAP
        q16 = sb("q16", [128, NPAIR, T], F16)
        QC = sb("QC", [128, QW], F16)
        par16 = sb("par16", [128, 2], F16)
        wkvT = sb("wkvT", [128, 2, NH, 2 * D], F16)
        c_in = sb("c_in", [KP, KT, D])
        cT = sb("cT", [128, 2, NH, M], F16)
        arena = sb("arena", [128, NPAIR * M + CH * 2 * CW], F16)
        KS = arena[:, 0:NPAIR * M].rearrange("p (i n) -> p i n", i=NPAIR)
        KN = arena[:, NPAIR * M:].rearrange("p (c a n) -> p c a n", c=CH, a=2)
        V = sb("V", [KP, KT, D])
        P = sb("P", [TP, 2, M])
        PT_all = sb("PT_all", [128, NPAIR, KT * TP])
        PT = PT_all[0:KP]
        qn = PT_all[:, 6:8, 0:T].bitcast(F16).rearrange("p h (a t) -> p h a t", a=2)
        hn, th, hg = (PT_all[0:TP, k, 0:TT * I].rearrange("p (t i) -> p t i", t=TT) for k in (4, 5, 6))
        hn_e, th_e, hg_e = (PT_all[:, 7, k * I:(k + 1) * I] for k in range(3))
        mx = sb("mx", [TP, NPAIR, 4])
        nmx = sb("nmx", [TP, NPAIR])
        den = sb("den", [TP, NPAIR])
        den_all = sb("den_all", [TP, B * NPAIR])
        oe = sb("oe", [128, 2, S])
        OT = sb("OT", [128, 2, T])
        dT = sb("dT", [NPAIR, B * TP])
        rd = sb("rd", [TP, TT, H])
        x1 = sb("x1", [TP, TT, D])
        xT = qT
        at = [0]

        def over_keys(rows, *shape):
            n = 1
            for k in shape:
                n *= k
            at[0] += n
            assert at[0] <= LATE <= NPAIR * M + CH * 2 * CW
            names = "abc"[:len(shape)]
            return arena[0:rows, at[0] - n:at[0]].rearrange(
                f"p ({' '.join(names)}) -> p {' '.join(names)}", **dict(zip(names, shape)))

        xT16 = over_keys(128, 2, NH, T)
        gateT = sb("gateT", [128, NH, E])
        r = [sb(f"r{i}", [TP, TT, E]) for i in range(8)]
        rs = [sb(f"rs{i}", [TP, TT]) for i in range(2)]
        sel16 = sb("sel16", [TP, TT, E], F16)
        shared_w = sb("shared_w", [TP, 1])
        slots = sb("slots", [TP, CAP])
        place = sb("place", [TP, E * TT])
        wt16 = sb("wt16", [TP, TT, E, 2], F16)
        slot_w = sb("slot_w", [CAP, 1])
        zero16 = sb("zero16", [TP, 512], F16)
        w13_in = [sb(f"w13_in{i}", [IH, 4, D]) for i in range(2)]
        w2_in = [sb(f"w2_in{i}", [128, NH, I]) for i in range(2)]
        w13T = [over_keys(128, 2, NH, 2 * I) for i in range(2)]
        w2T = [over_keys(IH, 2, 2 * D) for i in range(2)]
        hT = over_keys(IH, 2, 2, 2 * 2 * TP)
        x16 = over_keys(TP, TT, 2, D)
        sel = [over_keys(TP, TT, CAP) for i in range(2)]
        xeT = over_keys(128, 2, NH, CAP)
        selT = [over_keys(CAP, T) for i in range(2)]
        y16 = over_keys(CAP, 2, D)
        heT = over_keys(IH, 2, 2 * CAP)
        y_out = xn

        PS = stack.enter_context(nc.psum_tensor("PS", [128, 8, 512], F32))

        def bank16(b):
            return PS[:, b, :].bitcast(F16)

        names = """consts var_ready rstd_ready sp_ready x_loaded wq_loaded wp_loaded wkv_loaded small_loaded xq_ready wqq_ready wpq_ready
            sx_diag sp_diag pe_pre act_pre dve_pre qn_ready q_stacked0 q_stacked1 stack0 stack1 dve_step
            t_ready th_done tl_done k0_ready kh0_done kl0_done k1_ready kh1_done kl1_done
            qc0_done qc1_done sc_ready max_done exp_done tr_ready pt_act pt_dve v_ready v_act pv_ready o_done den_saved
            pe_post act_post dve_post pe_weights act_weights rden_ready rd_ready xb_ready
            oq_done oqt_done oqc_done proj_done ln_done lnt_done lnc_done
            shared_gu shared_tanh shared_h shared_ht shared_hh shared_hl shared_y added_init x16_ready
            w2t_ready w2h_done w2l_done w13t_ready w13h_done w13l_done
            sel_done xg_ready xg_done st_ready st_done slot_w_done
            gu_ready tanh_done h_done ht_ready hh_done hl_done y_ready yh_done yl_done added
            y_final stored""".split()
        s = {n: sem(n) for n in names}
        credited = names[names.index("t_ready"):names.index("den_saved") + 1] + names[names.index("w2t_ready"):names.index("added") + 1]

        def after(eng, name, n):
            eng.wait_ge(s[name], n + 1)

        ctx_in = [sem(f"ctx_in{c}") for c in range(CH)]
        w_in = [sem(f"w_in{i}") for i in range(2)]

        ctx_v = ctx.rearrange("b (p t) d -> b p t d", t=KT)
        w13_v = [w.rearrange("e (r p) d -> e p r d", p=IH) for w in (W1, W3)]
        w2_v = W2.rearrange("e (r p) i -> e p r i", p=128)
        v_bank = (7, 7, 6, 6, 6, 7)
        v0_bank = (7, 6, 7, 6, 7, 6)
        t_bank = (6, 7, 6, 7, 6, 6)
        t0_bank = (2, 3, 4, 5, 6, 0)
        k0_bank = (4, 5, 6)
        k_bank = ((7, 7, 6), (6, 7, 7))
        out_bank = (3, 6)
        proj_bank = (2, 6)
        o_bank = (7, 6)
        g_bank = (2, 3, 6, 2)
        h_bank = (3, 2)
        order = (2, 0, 1)
        block = stack.enter_context(nc.Block())

        def permuted(src):
            return src.rearrange("(j r) d -> r j d", r=PW)

        @block.sync
        def _(sp):
            sp.dma_start(x_in[:], x.rearrange("b s d -> (b s) d").rearrange("(t p) d -> p t d", p=TP)).then_inc(s["x_loaded"], 16)
            for k in range(NH):
                sp.dma_start(wkv_in[:, k, :], permuted(wkv[k * 128:(k + 1) * 128, :])).then_inc(s["wkv_loaded"], 16)
            sp.dma_start(wkv_in[:, NH:, :], wkv[D:, :].rearrange("(r p) d -> p r d", p=128)).then_inc(s["wkv_loaded"], 16)
            for c in range(CH):
                sp.dma_start(c_in[:, 4 * c:4 * c + 4, :], ctx_v[0, :, 4 * c:4 * c + 4, :]).then_inc(ctx_in[c], 16)
                if c == 0:
                    for k in range(NH):
                        sp.dma_start(wq_in[:, k, :], permuted(wq[k * 128:(k + 1) * 128, :])).then_inc(s["wq_loaded"], 16)
            sp.dma_start(wp_in[:], wp.rearrange("(r p) d -> p r d", p=128)).then_inc(s["wp_loaded"], 16)

            def next_load(n, c):
                after(sp, "t_ready", n * 6 + (2 * c + 2 - 6))
                sp.dma_start(c_in[:, 4 * c:4 * c + 4, :], ctx_v[n, :, 4 * c:4 * c + 4, :]).then_inc(ctx_in[c], 16)

            def stack_keys(n, oh, c, first=False):
                after(sp, f"kh{oh}_done", n * 3 + c + 1)
                if c == 0 and oh == 1:
                    after(sp, "sc_ready", n * SCN)
                elif c == 0 and not first:
                    after(sp, "sc_ready", n * SCN - SCN // 2)
                for a in range(2):
                    if a == 1:
                        after(sp, f"kl{oh}_done", n * 3 + c + 1)
                    for k in (a, a + 2):
                        sp.dma_start(KS[PW * k:PW * k + PW, 4 * oh:4 * oh + 4, c * CW:(c + 1) * CW], KN[:, c, a, :]).then_inc(s[f"stack{oh}"], 16)

            for c in range(CH):
                stack_keys(0, 0, c, first=True)
            for c in range(CH):
                next_load(1, c)

            def sp_sequence(b, load_next):
                for c in range(CH):
                    stack_keys(b, 1, c)
                stack_keys(b + 1, 0, 0)
                if load_next:
                    next_load(b + 2, 0)
                    next_load(b + 2, 1)
                stack_keys(b + 1, 0, 1)
                stack_keys(b + 1, 0, 2)
                if load_next:
                    next_load(b + 2, 2)

            with sp.Fori(0, B - 2) as b:
                sp_sequence(b, True)
            sp_sequence(B - 2, False)
            for c in range(CH):
                stack_keys(B - 1, 1, c)

            def load(e, q, srcs):
                for k in range(2):
                    sp.dma_start(w13_in[q][:, 2 * k:2 * k + 2, :], srcs[k]).then_inc(w_in[q], 16)
                sp.dma_start(w2_in[q][:], srcs[2]).then_inc(w_in[q], 16)

            load(E, 1, (Ws1.rearrange("(r p) d -> p r d", p=IH), Ws3.rearrange("(r p) d -> p r d", p=IH),
                        Ws2.rearrange("(r p) i -> p r i", p=128)))
            load(0, 0, (w13_v[0][0], w13_v[1][0], w2_v[0]))
            after(sp, "w13t_ready", 1)
            after(sp, "w2t_ready", 1)
            load(1, 1, (w13_v[0][1], w13_v[1][1], w2_v[1]))
            with sp.Fori(1, E // 2) as it:
                for q in range(2):
                    for name in ("w13t_ready", "w2t_ready"):
                        after(sp, name, it * 2 + q)
                    load(None, q, (w13_v[0][it * 2 + q], w13_v[1][it * 2 + q], w2_v[it * 2 + q]))
            sp.wait_ge(s["y_final"], 1)
            sp.dma_start(out.rearrange("b s d -> (b s) d").rearrange("(t p) d -> p t d", p=TP), y_out[:]).then_inc(s["stored"], 16)
            sp.wait_ge(s["stored"], 16)

        @block.gpsimd
        def _(gp):
            for name in credited:
                gp.sem_inc(s[name], 1)
            c = Steps(gp, s["consts"])
            for t, v in ((ident, 0.0), (ident16, 0.0), (ones, 1.0), (ones16, 1.0), (before16, 1.0), (hm2, 1.0),
                         (zero16, 0.0), (mhalf, -0.5)):
                c.did(gp.memset(t[:], v))
            c.did(gp.iota(rank[:], [[0, TT], [-1, E]], base=E, channel_multiplier=0, allow_small_or_imprecise_dtypes=True))
            c.did(gp.iota(slots[:], [[1, CAP]], base=0, channel_multiplier=0, allow_small_or_imprecise_dtypes=True))
            c.did(gp.memset(shared_w[:], 0.5 / FS ** 2))
            c.settle()
            for t in (ident, ident16):
                c.did(gp.affine_select(out=t[:], in_=t[:], compare_op=ALU.not_equal, fill=1.0, base=0,
                                       pattern=[[-1, 128]], channel_multiplier=1))
            c.did(gp.affine_select(out=before16[:], in_=before16[:], compare_op=ALU.is_ge, fill=0.0, base=-1,
                                   pattern=[[1, TP]], channel_multiplier=-1))
            c.did(gp.affine_select(out=hm2[:], in_=hm2[:], compare_op=ALU.is_ge, fill=0.0, base=0,
                                   pattern=[[-64, 2], [-16, 4]], channel_multiplier=1))
            c.settle()
            c.did(gp.affine_select(out=hm2[:], in_=hm2[:], compare_op=ALU.is_ge, fill=0.0, base=DH - 1,
                                   pattern=[[64, 2], [16, 4]], channel_multiplier=-1))
            c.settle()
            c.did(gp.tensor_tensor(hmask[:], hm2[:, 0, :], hm2[:, 1, :], ALU.add))
            c.settle()
            c.did(gp.tensor_tensor(par[:], hmask[:, 0:2], hmask[:, 2:4], ALU.add))
            c.settle()
            c.did(gp.tensor_copy(par16[:], par[:]))
            c.settle()
            gp.wait_ge(s["var_ready"], 1)
            gp.tensor_tensor(rstd[:], var[:], mhalf[:], ALU.pow).then_inc(s["rstd_ready"], 1)
            for t, src in ((bq_c, bq), (bk_c, bkv[0:D])):
                for k in range(NH):
                    gp.dma_start(t[:, k:k + 1], permuted(src[k * 128:(k + 1) * 128].unsqueeze(1)),
                                  allow_slow_non_contiguous=True).then_inc(s["small_loaded"], 16)
            for t, src in ((bv_r, bkv[D:2 * D].partition_broadcast(TP)), (bp_r, bp.partition_broadcast(TP)),
                           (gb_r, gate_b.partition_broadcast(TP))):
                gp.dma_start(t[:], src, allow_slow_non_contiguous=True).then_inc(s["small_loaded"], 16)
            gp.dma_start(gate_in[:], gate_w).then_inc(s["small_loaded"], 16)
            for k, g in enumerate((g_xattn, g_ffn)):
                gp.dma_start(gx[:, k:k + 1], g.partition_broadcast(TP)).then_inc(s["small_loaded"], 16)
            for oh in range(NH):
                for k in range(4):
                    gp.wait_ge(s["qn_ready"], 1 + k // 2)
                    gp.dma_start(q16[PW * k:PW * k + PW, 4 * oh:4 * oh + 4, :], qn[:, oh, k // 2, :]).then_inc(s[f"q_stacked{oh}"], 16)

            def queries(n, k):
                gp.tensor_tensor(QC[:, k * (QW // 2):(k + 1) * (QW // 2)].rearrange("p (i a n) -> p i a n", i=4, a=2),
                                 q16[:, 4 * k:4 * k + 4, bass.ds(n * S, S)].unsqueeze(2).to_broadcast([128, 4, 2, S]),
                                 par16[:].unsqueeze(1).unsqueeze(3).to_broadcast([128, 4, 2, S]), ALU.mult).then_inc(s[f"qc{k}_done"], 1)

            def sums(b):
                after(gp, "exp_done", b * NPAIR + NPAIR)
                gp.tensor_copy(den_all[:, bass.ds(b * NPAIR, NPAIR)], den[:]).then_inc(s["den_saved"], 1)

            for k in range(2):
                gp.wait_ge(s[f"q_stacked{k}"], 16 * 4)
                queries(0, k)
            gp.wait_ge(s["act_pre"], 5)
            gp.wait_ge(s["small_loaded"], NSMALL)
            gp.wait_ge(s["x_loaded"], 16)
            gp.tensor_tensor(bp_r[:], bp_r[:], tg[:, 0:1].to_broadcast([TP, D]), ALU.mult).then_inc(s["xb_ready"], 1)
            gp.wait_ge(s["xb_ready"], 1)
            gp.tensor_tensor(x1[:], x_in[:], bp_r[:].unsqueeze(1).to_broadcast([TP, TT, D]), ALU.add).then_inc(s["xb_ready"], 1)
            with gp.Fori(0, B - 1) as b:
                for k in range(2):
                    after(gp, "sc_ready", b * SCN + (k + 1) * (SCN // 2))
                    queries(b + 1, k)
                sums(b)
            sums(B - 1)
            for k in range(2):
                gp.wait_ge(s["var_ready"], 2 + k)
                gp.tensor_tensor(rstd[:, 2 * k:2 * k + 2], var[:, 2 * k:2 * k + 2], mhalf[:, 2 * k:2 * k + 2], ALU.pow).then_inc(s["rstd_ready"], 1)
            gp.memset(selT[1], 0.0).then_inc(s["added_init"], 1)
            gp.memset(y16[:], 0.0).then_inc(s["added_init"], 1)
            gp.wait_ge(s["act_post"], 6)
            gp.tensor_tensor(x16[:, :, 1], xn[:], x16[:, :, 0], ALU.subtract).then_inc(s["x16_ready"], 1)

        @block.scalar
        def _(act):
            ap = Steps(act, s["act_pre"])
            act.wait_ge(s["pe_pre"], 1)
            ap.did(act.activation(wkvT[:, 0], PS[:, 0:2, :], ACT.Copy, scale=WS))

            def context_hi(n, u, b=None):
                c, hf = divmod(u, 2)
                bank = (t0_bank if b is None else t_bank)[u]
                after(act, "t_ready", n * 6 + u + 1)
                if b is not None and hf == 0:
                    after(act, "v_ready", b * 6 + 2 * c + 2)
                    after(act, "k1_ready", b * 3 + c + 1)
                act.activation(cT[:, 0, hf, c * CW:(c + 1) * CW], PS[:, bank, 0:CW], ACT.Copy).then_inc(s["th_done"], 1)

            def keys_hi(n, oh, c, bank=None):
                after(act, f"k{oh}_ready", n * 3 + c + 1)
                if c == 0 and bank is None:
                    act.wait_ge(s[f"stack{1 - oh}"], n * STACKED + (STACKED if oh == 1 else 0))
                act.activation(KN[:, c, 0, :], PS[:, bank or k_bank[oh][c], 0:CW], ACT.Identity,
                               bias=bk_c[:, oh:oh + 1]).then_inc(s[f"kh{oh}_done"], 1)

            def evacuate_values(b, v, bank):
                after(act, "v_ready", b * 6 + v + 1)
                act.activation(V[:, 2 * v:2 * v + 2, :].rearrange("p t d -> p (t d)"), PS[0:KP, bank, :], ACT.Copy).then_inc(s["v_act"], 1)

            def act_sequence(b, prepare, first=False):
                n = b + 1

                def v_evac(v):
                    if not first:
                        evacuate_values(b, v, v_bank[v])

                def exp(i):
                    after(act, "max_done", b * NPAIR + i + 1)
                    after(act, "tr_ready", b * NPAIR + max(i - 1, 0))
                    act.activation(P[:, i % 2, :].rearrange("p (c k) -> p c k", c=CH),
                                   PS[0:TP, 3 * (i % 2):3 * (i % 2) + 3, 0:CW], ACT.Exp, bias=nmx[:, i:i + 1],
                                   scale=SCORE, accum_out=den[:, i:i + 1]).then_inc(s["exp_done"], 1)

                def pt_evac(i):
                    after(act, "tr_ready", b * NPAIR + i + 1)
                    act.activation(PT[:, i, 0:8 * TP].rearrange("p (c k) -> p c k", c=2),
                                   PS[0:KP, 3 * (i % 2):3 * (i % 2) + 2, 0:4 * TP], ACT.Copy).then_inc(s["pt_act"], 1)

                def next_context(*units):
                    if prepare:
                        for u in units:
                            context_hi(n, u, b)

                def next_keys(c):
                    if prepare:
                        keys_hi(n, 0, c)

                after(act, "pv_ready", b * 2)
                v_evac(0)
                keys_hi(b, 1, 0)
                after(act, "den_saved", b)
                exp(0)
                v_evac(1)
                next_context(0)
                pt_evac(0)
                keys_hi(b, 1, 1)
                exp(1)
                v_evac(2)
                keys_hi(b, 1, 2)
                pt_evac(1)
                exp(2)
                v_evac(3)
                next_context(1)
                pt_evac(2)
                exp(3)
                v_evac(4)
                next_keys(0)
                next_context(2)
                exp(4)
                next_context(3)
                pt_evac(3)
                pt_evac(4)
                next_keys(1)
                exp(5)
                v_evac(5)
                next_context(4)
                pt_evac(5)
                exp(6)
                next_context(5)
                exp(7)
                next_keys(2)
                pt_evac(6)
                pt_evac(7)

            for u in range(5):
                context_hi(0, u)
            act.wait_ge(s["pe_pre"], 2)
            ap.did(act.activation(xqT[:], bank16(7)[:, 0:NH * T].rearrange("p (h t) -> p h t", h=NH), ACT.Copy))
            act.wait_ge(s["pe_pre"], 3)
            ap.did(act.activation(sx_row[:], PS[:, 1, 0:T], ACT.Copy))
            context_hi(0, 5)
            act.wait_ge(s["pe_pre"], 4)
            ap.did(act.activation(wqT[:], bank16(7)[:, 0:NH * D].rearrange("p (h t) -> p h t", h=NH), ACT.Copy))
            act.wait_ge(s["small_loaded"], NSMALL)
            ap.did(act.activation(tg[:, 0:1], gx[:, 0:1], ACT.Tanh))
            ap.did(act.activation(bk_c[:], bk_c[:], ACT.Copy, scale=WS))
            act.wait_ge(s["act_pre"], 6)
            for c in range(CH):
                keys_hi(0, 0, c, bank=k0_bank[c])
            for v in range(6):
                evacuate_values(0, v, v0_bank[v])
            act_sequence(0, True, first=True)
            with act.Fori(1, B - 1) as b:
                act_sequence(b, True)
            act_sequence(B - 1, False)

            def weights_hi(n, q):
                after(act, "w2t_ready", n)
                act.activation(w2T[q][:, 0], PS[0:IH, 7, :], ACT.Copy, scale=FS).then_inc(s["w2h_done"], 1)
                after(act, "w13t_ready", n)
                act.activation(w13T[q][:, 0], PS[:, 4:6, 0:2 * I], ACT.Copy, scale=FS).then_inc(s["w13h_done"], 1)

            act.wait_ge(s["pe_post"], 1)
            dT_w = dT[:].rearrange("p (a b n) -> p b a n", a=2, b=B)
            for k in range(2):
                last = act.activation(dT_w[:, 4 * k:4 * k + 4], PS[0:NPAIR, k, 0:4 * TP].rearrange("p (b a n) -> p b a n", b=4, a=2),
                                      ACT.Copy, scale=1.0 / WS)
            last.then_inc(s["act_post"], 1)
            act.wait_ge(s["pe_post"], 2)
            act.activation(rd[:].rearrange("p t (i a) -> p t a i", a=2), PS[0:TP, 2, 0:TT * H].rearrange("p (t a i) -> p t a i", t=TT, a=2),
                           ACT.Copy).then_inc(s["rd_ready"], 1)
            act.wait_ge(s["pe_weights"], 1)
            act.activation(gateT[:], PS[:, 0, 0:NH * E].rearrange("p (h e) -> p h e", h=NH), ACT.Copy).then_inc(s["act_weights"], 1)
            act.wait_ge(s["pe_weights"], 2)
            act.activation(wpT[:], bank16(1)[:, 0:NH * D].rearrange("p (h t) -> p h t", h=NH), ACT.Copy).then_inc(s["act_weights"], 1)
            act.activation(sp_row[:], PS[0:TP, 1, D:2 * D], ACT.Copy, scale=tg[0:TP, 0:1]).then_inc(s["act_weights"], 1)
            weights_hi(1, 1)
            for k in range(2):
                act.wait_ge(s["oqt_done"], k + 1)
                act.activation(xqT[:, :, 2 * k * TP:2 * (k + 1) * TP], bank16(1 - k)[:, 0:NH * 2 * TP].rearrange("p (h t) -> p h t", h=NH),
                               ACT.Copy).then_inc(s["oqc_done"], 1)
            for k in range(2):
                act.wait_ge(s["lnt_done"], k + 1)
                act.activation(xT[:, :, 2 * k * TP:2 * (k + 1) * TP], PS[:, k, 0:NH * 2 * TP].rearrange("p (h t) -> p h t", h=NH),
                               ACT.Copy).then_inc(s["lnc_done"], 1)
            act.activation(xT16[:, 0].rearrange("p h (k t) -> p h k t", k=2), PS[:, 0:2, 0:NH * 2 * TP].rearrange("p k (h t) -> p h k t", h=NH),
                           ACT.Copy).then_inc(s["act_post"], 1)
            act.wait_ge(s["dve_post"], 3)
            act.activation(r[1][:], r[2][:], ACT.Exp).then_inc(s["act_post"], 1)
            for t in range(TT):
                act.wait_ge(s["shared_gu"], t + 1)
                act.activation(th[:, t, :], PS[0:TP, g_bank[t], 0:I], ACT.Tanh, scale=0.5 / FS).then_inc(s["shared_tanh"], 1)
                if t == 1:
                    act.wait_ge(s["sp_ready"], 1)
                    act.activation(r[4][:], r[5][:], ACT.Sqrt).then_inc(s["act_post"], 1)
            act.activation(tg[:, 1:2], gx[:, 1:2], ACT.Tanh).then_inc(s["act_post"], 1)
            act.activation(x16[:, :, 0], xn[:], ACT.Copy).then_inc(s["act_post"], 1)
            for p in range(2):
                act.wait_ge(s["shared_ht"], p + 1)
                act.activation(hT[:, 0, p, :], PS[0:IH, h_bank[p], 0:4 * TP], ACT.Copy).then_inc(s["shared_hh"], 1)
            weights_hi(2, 0)

            def tokens_hi(e):
                after(act, "xg_ready", e + 1)
                act.activation(xeT[:].rearrange("p a h c -> p (a h c)"), PS[:, 3, 0:4 * CAP], ACT.Copy).then_inc(s["xg_done"], 1)

            def slots_turned(e, q):
                after(act, "st_ready", e + 1)
                after(act, "added", e)
                act.activation(selT[q], bank16(6)[:, 0:T], ACT.Copy).then_inc(s["st_done"], 1)

            def expert(e, q, prepare):
                after(act, "gu_ready", e + 1)
                after(act, "h_done", e)
                act.activation(th_e, PS[:, 6, 0:I], ACT.Tanh, scale=0.5 / FS).then_inc(s["tanh_done"], 1)
                after(act, "y_ready", e)
                if prepare:
                    weights_hi(e + 3, 1 - q)
                after(act, "ht_ready", e + 1)
                act.activation(heT[:, 0, :], PS[0:IH, 2, 0:2 * CAP], ACT.Copy).then_inc(s["hh_done"], 1)
                if prepare:
                    tokens_hi(e + 1)
                    slots_turned(e + 1, 1 - q)
                after(act, "y_ready", e + 1)
                after(act, "added", e + 1)
                act.activation(y16[:, 0, :], PS[:, 2, 0:D], ACT.Copy, scale=1.0 / FS).then_inc(s["yh_done"], 1)

            act.wait_ge(s["added_init"], 2)
            act.wait_ge(s["shared_y"], 2)
            tokens_hi(0)
            slots_turned(0, 0)
            with act.Fori(0, E // 2 - 1) as it:
                for q in range(2):
                    expert(it * 2 + q, q, True)
            expert(E - 2, 0, True)
            expert(E - 1, 1, False)

        @block.vector
        def _(dve):
            d = Steps(dve, s["dve_step"])

            def quantise(src, n, am_, s_, out16, k=d):
                k.settle()
                k.did(dve.tensor_reduce(am_[:, 0:n], src[:], AX.X, ALU.max, apply_absolute_value=True))
                k.settle()
                k.did(dve.tensor_scalar(s_[:], am_[:, 0:n], 1.0 / 127, 1e-8, ALU.mult, ALU.max))
                k.settle()
                k.did(dve.reciprocal(am_[:, 0:n], s_[:]))
                k.settle()
                for r_ in range(n):
                    k.did(dve.tensor_scalar(src[:, r_, :], src[:, r_, :], am_[:, r_:r_ + 1], 127.0, ALU.mult, ALU.min))
                k.settle()
                k.did(dve.tensor_scalar(src[:], src[:], -127.0, MAGIC, ALU.max, ALU.add))
                k.settle()
                return dve.tensor_scalar(out16[:], src[:], MAGIC, None, ALU.subtract)

            def context_lo(n, u, bank=None):
                c, hf = divmod(u, 2)
                after(dve, "th_done", n * 6 + u + 1)
                dve.tensor_tensor(cT[:, 1, hf, c * CW:(c + 1) * CW], PS[:, t_bank[u] if bank is None else bank, 0:CW],
                                  cT[:, 0, hf, c * CW:(c + 1) * CW], ALU.subtract).then_inc(s["tl_done"], 1)

            def statistics(src, tiles):
                d.settle()
                for t in tiles:
                    d.did(dve.bn_stats(st[:, t, :], src[:, t, :]))
                d.settle()
                for t in tiles:
                    d.did(dve.bn_aggr(mv[:, t, :], st[:, t, :]))
                d.settle()
                part = slice(tiles[0], tiles[-1] + 1)
                dve.tensor_scalar(var[:, part], mv[:, part, 1], EPS, None, ALU.add).then_inc(s["var_ready"], 1)

            def normalise(src, dst, tiles, nth):
                dve.wait_ge(s["rstd_ready"], nth)
                for t in tiles:
                    last = dve.tensor_scalar(dst[:, t, :], src[:, t, :], mv[:, t, 0:1], rstd[:, t:t + 1], ALU.subtract, ALU.mult)
                return last

            dve.wait_ge(s["x_loaded"], 16)
            statistics(x_in, range(TT))
            d.did(normalise(x_in, xn, range(TT), 1))
            quantise(xn, TT, am[0:TP], sx, xq16).then_inc(s["xq_ready"], 1)
            dve.wait_ge(s["consts"], NCONST)
            for t in range(TT):
                last = dve.tensor_scalar(diag[0:TP, t, 0:TP], ident[0:TP, 0:TP], sx[:, t:t + 1], None, ALU.mult)
            last.then_inc(s["sx_diag"], 1)
            dve.wait_ge(s["act_pre"], 1)
            dve.scalar_tensor_tensor(wkvT[:, 1], PS[:, 0:2, :], WS, wkvT[:, 0], ALU.mult, ALU.subtract).then_inc(s["dve_pre"], 1)
            dve.wait_ge(s["wq_loaded"], 16 * NH)
            quantise(wq_in, NH, am, swq, wq16).then_inc(s["wqq_ready"], 1)
            for u in range(6):
                context_lo(0, u, t0_bank[u])
            dve.wait_ge(s["small_loaded"], NSMALL)
            dve.wait_ge(s["act_pre"], 3)
            dve.wait_ge(s["pe_pre"], 5)
            for oh in range(NH):
                d.did(dve.scalar_tensor_tensor(qT[:, oh, :], PS[:, 2 + oh, 0:T], swq[:, oh:oh + 1], sx_row[:], ALU.mult, ALU.mult))
            d.settle()
            for oh in range(NH):
                d.did(dve.tensor_scalar(qT[:, oh, :], qT[:, oh, :], bq_c[:, oh:oh + 1], None, ALU.add))
            d.settle()
            dve.tensor_copy(qn[:, :, 0, :], qT[:]).then_inc(s["qn_ready"], 1)
            dve.wait_ge(s["qn_ready"], 1)
            dve.tensor_tensor(qn[:, :, 1, :], qT[:], qn[:, :, 0, :], ALU.subtract).then_inc(s["qn_ready"], 1)
            pre_steps = d.n

            def keys_lo(n, oh, c, bank=None):
                after(dve, f"kh{oh}_done", n * 3 + c + 1)
                dve.scalar_tensor_tensor(KN[:, c, 1, :], PS[:, bank or k_bank[oh][c], 0:CW], bk_c[:, oh:oh + 1],
                                         KN[:, c, 0, :], ALU.add, ALU.subtract).then_inc(s[f"kl{oh}_done"], 1)

            def dve_sequence(b, prepare):
                n = b + 1
                step = Steps(dve, s["dve_step"], b * SEQ_STEPS + pre_steps)

                def row_max(i):
                    for k, c in enumerate(order):
                        after(dve, "sc_ready", b * SCN + i * CH + k + 1)
                        step.did(dve.tensor_reduce(mx[:, i, c:c + 1], PS[0:TP, 3 * (i % 2) + c, 0:CW], AX.X, ALU.max))
                    step.settle()
                    step.did(dve.scalar_tensor_tensor(mx[:, i, 3:4], mx[:, i, 0:1], mx[:, i, 1:2], mx[:, i, 2:3], ALU.max, ALU.max))
                    step.settle()
                    dve.tensor_scalar(nmx[:, i:i + 1], mx[:, i, 3:4], -SCORE, None, ALU.mult).then_inc(s["max_done"], 1)

                def pt_evac(i):
                    after(dve, "tr_ready", b * NPAIR + i + 1)
                    dve.tensor_copy(PT[:, i, 8 * TP:KT * TP], PS[0:KP, 3 * (i % 2) + 2, 0:4 * TP]).then_inc(s["pt_dve"], 1)

                def o_evac(gh):
                    after(dve, "pv_ready", b * 2 + gh + 1)
                    step.did(dve.tensor_scalar(oe[:, gh], PS[:, o_bank[gh], 0:S], par[:, 0:1], None, ALU.mult))
                    step.settle()
                    dve.scalar_tensor_tensor(OT[:, gh, bass.ds(b * S, S)], PS[:, o_bank[gh], S:2 * S], par[:, 1:2], oe[:, gh],
                                             ALU.mult, ALU.add).then_inc(s["o_done"], 1)

                after(dve, "pv_ready", b * 2)
                after(dve, "exp_done", b * NPAIR)

                def next_context(*units):
                    if prepare:
                        for u in units:
                            context_lo(n, u)

                def next_keys(c):
                    if prepare:
                        keys_lo(n, 0, c)

                row_max(0)
                keys_lo(b, 1, 0)
                row_max(1)
                next_context(0)
                pt_evac(0)
                keys_lo(b, 1, 1)
                row_max(2)
                keys_lo(b, 1, 2)
                pt_evac(1)
                row_max(3)
                pt_evac(2)
                next_context(1)
                row_max(4)
                next_keys(0)
                next_context(2)
                pt_evac(3)
                next_context(3)
                pt_evac(4)
                row_max(5)
                next_keys(1)
                row_max(6)
                pt_evac(5)
                next_context(4)
                row_max(7)
                next_context(5)
                pt_evac(6)
                next_keys(2)
                if not prepare:
                    dve.wait_ge(s["wp_loaded"], 16)
                    quantise(wp_in, NH, am, swp, wp16, step).then_inc(s["wpq_ready"], 1)
                    for k in range(NH):
                        last = dve.tensor_scalar(diag[:, k, :], ident[:], swp[:, k:k + 1], None, ALU.mult)
                    last.then_inc(s["sp_diag"], 1)
                pt_evac(7)
                if not prepare:
                    after(dve, "den_saved", B)
                    dve.reciprocal(den_all[:], den_all[:]).then_inc(s["rden_ready"], 1)
                o_evac(0)
                o_evac(1)
                assert step.n == SEQ_STEPS + (0 if prepare else WP_STEPS)

            for c in range(CH):
                keys_lo(0, 0, c, bank=k0_bank[c])
            with dve.Fori(0, B - 1) as b:
                dve_sequence(b, True)
            dve_sequence(B - 1, False)

            d.base = B * SEQ_STEPS + WP_STEPS
            pn = [0]

            def post(ins):
                pn[0] += 1
                ins.then_inc(s["dve_post"], 1)

            def w2_lo(n, q):
                after(dve, "w2h_done", n)
                dve.scalar_tensor_tensor(w2T[q][:, 1], PS[0:IH, 7, :], FS, w2T[q][:, 0], ALU.mult, ALU.subtract).then_inc(s["w2l_done"], 1)

            def w13_lo(n, q):
                after(dve, "w13h_done", n)
                dve.scalar_tensor_tensor(w13T[q][:, 1], PS[:, 4:6, 0:2 * I], FS, w13T[q][:, 0], ALU.mult, ALU.subtract).then_inc(s["w13l_done"], 1)

            dve.wait_ge(s["pe_post"], 3)
            dve.wait_ge(s["rd_ready"], 1)
            for k in range(2):
                pair = slice(2 * k, 2 * k + 2)
                d.did(dve.tensor_tensor(xn[:, pair, :].rearrange("p t (h j) -> p t h j", h=H),
                                        PS[0:TP, out_bank[k], :].rearrange("p (t h j) -> p t h j", t=2, h=H),
                                        rd[:, pair, :].unsqueeze(3).to_broadcast([TP, 2, H, DH]), ALU.mult))
                d.settle()
                d.did(dve.tensor_tensor(xn[:, pair, :], xn[:, pair, :], bv_r[:].unsqueeze(1).to_broadcast([TP, 2, D]), ALU.add))
                quantise(xn[:, pair, :], 2, am[0:TP], so[:, pair], xq16[:, pair, :]).then_inc(s["oq_done"], 1)
            w2_lo(1, 1)
            w13_lo(1, 1)
            dve.wait_ge(s["act_weights"], 3)
            dve.wait_ge(s["xb_ready"], 2)
            dve.wait_ge(s["oq_done"], 2)
            for k in range(2):
                pair = slice(2 * k, 2 * k + 2)
                dve.wait_ge(s["proj_done"], k + 1)
                for t in range(2 * k, 2 * k + 2):
                    d.did(dve.scalar_tensor_tensor(xn[:, t, :], PS[0:TP, proj_bank[k], (t % 2) * D:(t % 2 + 1) * D], so[:, t:t + 1],
                                                   sp_row[:], ALU.mult, ALU.mult))
                d.settle()
                d.did(dve.tensor_tensor(x1[:, pair, :], x1[:, pair, :], xn[:, pair, :], ALU.add))
                statistics(x1, range(2 * k, 2 * k + 2))
            for k in range(2):
                normalise(x1, xn, range(2 * k, 2 * k + 2), 2 + k).then_inc(s["ln_done"], 1)
            dve.wait_ge(s["act_post"], 2)
            post(dve.tensor_tensor(xT16[:, 1], xT[:], xT16[:, 0], ALU.subtract))
            logit, e_, z, z2, acc, a, b_, c_ = (r[0], r[1], r[2], r[3], r[4], r[5], r[6], r[7])
            dve.wait_ge(s["pe_post"], 4)
            post(dve.tensor_copy(logit[:], PS[0:TP, 3, 0:TT * E].rearrange("p (t e) -> p t e", t=TT)))
            dve.wait_ge(s["dve_post"], 2)
            post(dve.scalar_tensor_tensor(z[:], logit[:], -1.0, logit[:], ALU.mult, ALU.min))
            dve.wait_ge(s["act_post"], 3)
            def one(ins):
                d.did(ins)
                d.settle()
            one(dve.tensor_scalar(a[:], e_[:], 2.0, None, ALU.add))
            one(dve.reciprocal(a[:], a[:]))
            one(dve.tensor_tensor(z[:], e_[:], a[:], ALU.mult))
            one(dve.tensor_tensor(z2[:], z[:], z[:], ALU.mult))
            one(dve.tensor_scalar(acc[:], z2[:], 2.0 / 17, None, ALU.mult))
            for k in (15, 13, 11, 9, 7, 5, 3):
                one(dve.scalar_tensor_tensor(acc[:], acc[:], 2.0 / k, z2[:], ALU.add, ALU.mult))
            one(dve.scalar_tensor_tensor(acc[:], acc[:], 2.0, z[:], ALU.add, ALU.mult))
            dve.scalar_tensor_tensor(a[:], logit[:], 0.0, acc[:], ALU.max, ALU.add).then_inc(s["sp_ready"], 1)
            def hidden(p):
                for t in range(2 * p, 2 * p + 2):
                    dve.wait_ge(s["shared_tanh"], t + 1)
                    d.did(dve.scalar_tensor_tensor(hg[:, t, :], th[:, t, :], 1.0, PS[0:TP, g_bank[t], 0:I], ALU.add, ALU.mult))
                    d.settle()
                    dve.scalar_tensor_tensor(hn[:, t, :], PS[0:TP, g_bank[t], I:2 * I], shared_w[:, 0:1], hg[:, t, :],
                                             ALU.mult, ALU.mult).then_inc(s["shared_h"], 1)

            hidden(0)
            dve.wait_ge(s["act_post"], 4)
            sc, bias = acc, z2
            one(dve.tensor_tensor(bias[:], sc[:], gb_r[:].unsqueeze(1).to_broadcast([TP, TT, E]), ALU.add))
            for k, oh in enumerate((e_, z)):
                one(dve.tensor_reduce(rs[0][:], bias[:], AX.X, ALU.max))
                one(dve.tensor_tensor(a[:], bias[:], rs[0][:].unsqueeze(2).to_broadcast([TP, TT, E]), ALU.is_ge))
                one(dve.tensor_tensor(a[:], a[:], rank[:], ALU.mult))
                one(dve.tensor_reduce(rs[0][:], a[:], AX.X, ALU.max))
                one(dve.tensor_tensor(oh[:], a[:], rs[0][:].unsqueeze(2).to_broadcast([TP, TT, E]), ALU.is_equal))
                if k == 0:
                    one(dve.scalar_tensor_tensor(bias[:], oh[:], -3e38, bias[:], ALU.mult, ALU.add))
                    hidden(1)
                if k == 1:
                    one(dve.tensor_tensor(c_[:], e_[:], z[:], ALU.add))
                    post(dve.tensor_copy(sel16[:], c_[:]))
                dve.wait_ge(s["shared_hh"], k + 1)
                dve.tensor_tensor(hT[:, 1, k, :], PS[0:IH, h_bank[k], 0:4 * TP], hT[:, 0, k, :], ALU.subtract).then_inc(s["shared_hl"], 1)
            one(dve.tensor_tensor(a[:], sc[:], c_[:], ALU.mult))
            one(dve.tensor_reduce(rs[1][:], a[:], AX.X, ALU.add))
            one(dve.reciprocal(rs[1][:], rs[1][:]))
            one(dve.tensor_tensor(a[:], a[:], rs[1][:].unsqueeze(2).to_broadcast([TP, TT, E]), ALU.mult))
            d.did(dve.tensor_copy(wt16[:, :, :, 0], a[:]))
            d.settle()
            d.did(dve.tensor_tensor(wt16[:, :, :, 1], a[:], wt16[:, :, :, 0], ALU.subtract))
            dve.wait_ge(s["pe_post"], 5)
            one(dve.scalar_tensor_tensor(b_[:], PS[0:TP, 6, 0:TT * E].rearrange("p (t e) -> p t e", t=TT), 1.0, c_[:], ALU.add, ALU.mult))
            post(dve.tensor_scalar(place[:].rearrange("p (e t) -> p t e", t=TT), b_[:], -1.0, None, ALU.add))
            dve.wait_ge(s["act_post"], 5)
            d.did(dve.tensor_scalar(tgf[:], tg[:, 1:2], 1.0 / FS, None, ALU.mult))
            d.settle()
            post_steps = d.n

            def select(e, q, first=False):
                if not first:
                    after(dve, "st_ready", e - 1)
                dve.tensor_tensor(sel[q], slots[:].unsqueeze(1).to_broadcast([TP, TT, CAP]),
                                  place[:, bass.ds(e * TT, TT)].unsqueeze(2).to_broadcast([TP, TT, CAP]),
                                  ALU.is_equal).then_inc(s["sel_done"], 1)

            def slot_weights(e):
                after(dve, "st_ready", e + 1)
                after(dve, "st_done", e + 1)
                after(dve, "h_done", e)
                dve.tensor_scalar(slot_w[:], PS[:, 6, W_COL:W_COL + 1], PS[:, 6, W_COL + 1:W_COL + 2], 0.5 / FS, ALU.add, ALU.mult).then_inc(s["slot_w_done"], 1)

            def expert(e, q, prepare):
                own = Steps(dve, s["dve_step"], e + (d.base + post_steps))
                if prepare:
                    select(e + 1, 1 - q)
                after(dve, "tanh_done", e + 1)
                after(dve, "h_done", e)
                own.did(dve.scalar_tensor_tensor(hg_e, th_e, 1.0, PS[:, 6, 0:I], ALU.add, ALU.mult))
                own.settle()
                after(dve, "ht_ready", e)
                after(dve, "slot_w_done", e + 1)
                dve.scalar_tensor_tensor(hn_e, PS[:, 6, I:2 * I], slot_w[:, 0:1], hg_e, ALU.mult, ALU.mult).then_inc(s["h_done"], 1)
                if prepare:
                    w2_lo(e + 3, 1 - q)
                after(dve, "hh_done", e + 1)
                dve.tensor_tensor(heT[:, 1, :], PS[0:IH, 2, 0:2 * CAP], heT[:, 0, :], ALU.subtract).then_inc(s["hl_done"], 1)
                if prepare:
                    w13_lo(e + 3, 1 - q)
                    slot_weights(e + 1)
                after(dve, "yh_done", e + 1)
                dve.scalar_tensor_tensor(y16[:, 1, :], PS[:, 2, 0:D], 1.0 / FS, y16[:, 0, :], ALU.mult, ALU.subtract).then_inc(s["yl_done"], 1)
                assert own.n == 1

            dve.wait_ge(s["dve_post"], 5)
            select(0, 0, first=True)
            w2_lo(2, 0)
            w13_lo(2, 0)
            slot_weights(0)
            with dve.Fori(0, E // 2 - 1) as it:
                for q in range(2):
                    expert(it * 2 + q, q, True)
            expert(E - 2, 0, True)
            expert(E - 1, 1, False)
            after(dve, "added", E + 1)
            for t in range(TT):
                last = dve.scalar_tensor_tensor(y_out[:, t, :], PS[0:TP, t // 2, (t % 2) * D:(t % 2 + 1) * D], tgf[:, 0:1], x1[:, t, :],
                                                ALU.mult, ALU.add)
            last.then_inc(s["y_final"], 1)

        @block.tensor
        def _(pe):
            mm, tp = pe.matmul, pe.transpose

            def split3(out_, w, x_, first=True, last=True, halves=2):
                todo = [(a, b, h) for a, b in SPLIT for h in range(halves)]
                for k, (a, b, h) in enumerate(todo):
                    ins = mm(out_, w(a, h), x_(b, h), start=first and k == 0, stop=last and k == len(todo) - 1)
                return ins

            pe.wait_ge(s["consts"], NCONST)
            pe.wait_ge(s["wkv_loaded"], 16 * (NH + 1))
            for h in range(NH):
                for k in range(2 * NH):
                    last = tp(PS[:, h, k * 128:(k + 1) * 128], wkv_in[:, k, h * 128:(h + 1) * 128], ident[:])
            last.then_inc(s["pe_pre"], 1)

            def context(n, u, b=None):
                c, hf = divmod(u, 2)
                if hf == 0:
                    pe.wait_ge(ctx_in[c], n * 16 + 16)
                if b is None:
                    if u == 5:
                        pe.wait_ge(s["dve_pre"], 1)
                elif u < 2:
                    after(pe, "kl1_done", b * 3 + (1, 3)[u])
                elif u == 2:
                    after(pe, "v_act", b * 6 + 5)
                elif u == 3:
                    after(pe, "kl0_done", n * 3 + 1)
                else:
                    after(pe, "tl_done", n * 6 + (3, 5)[u - 4])
                for j in range(4):
                    last = tp(PS[:, (t0_bank if b is None else t_bank)[u], j * KP:(j + 1) * KP], c_in[:, 4 * c + j, hf * 128:(hf + 1) * 128], ident[0:KP, 0:KP])
                last.then_inc(s["t_ready"], 1)

            def keys(n, oh, c, bank=None):
                if oh == 0:
                    after(pe, "tl_done", n * 6 + ((2, 4, 6) if bank is None else (3, 4, 6))[c])
                elif c == 0:
                    after(pe, "o_done", n * 2)
                elif c == 1:
                    after(pe, "v_act", n * 6 + 2)
                else:
                    after(pe, "kl1_done", n * 3 + 2)
                split3(PS[:, bank or k_bank[oh][c], 0:CW], lambda a, h: wkvT[:, a, h, oh * 128:(oh + 1) * 128],
                       lambda a, h: cT[:, a, h, c * CW:(c + 1) * CW]).then_inc(s[f"k{oh}_ready"], 1)

            def project_values(v, bank):
                for k in range(2):
                    t = 2 * v + k
                    last = split3(PS[0:KP, bank, k * D:(k + 1) * D], lambda a, h: cT[:, a, h, t * KP:(t + 1) * KP],
                                  lambda a, h: wkvT[:, a, h, D:2 * D])
                last.then_inc(s["v_ready"], 1)

            def pe_sequence(b, prepare, first=False):
                n = b + 1

                def scores(i):
                    if i % 4 == 0:
                        pe.wait_ge(s[f"stack{i // 4}"], b * STACKED + STACKED)
                        after(pe, f"qc{i // 4}_done", b + 1)
                    for c in order:
                        if c != 1:
                            after(pe, "pt_dve" if c == 2 else "pt_act", b * NPAIR + max(i - 1, 0))
                        last = mm(PS[0:TP, 3 * (i % 2) + c, 0:CW], QC[:, i * TP:(i + 1) * TP], KS[:, i, c * CW:(c + 1) * CW],
                                  start=True, stop=True)
                        last.then_inc(s["sc_ready"], 1)

                def values(v):
                    if v == 0:
                        after(pe, "v_act" if first else "o_done", 6 if first else b * 2)
                    elif v == 1:
                        after(pe, "v_act", b * 6 + 1)
                    elif v == 2:
                        if prepare:
                            after(pe, "tl_done", n * 6 + 1)
                        else:
                            after(pe, "kl1_done", b * 3 + 1)
                    elif v < 5:
                        after(pe, "v_act", b * 6 + v)
                    elif prepare:
                        after(pe, "kl0_done", n * 3 + 2)
                    else:
                        after(pe, "kl1_done", b * 3 + 3)
                    if not first:
                        project_values(v, v_bank[v])

                def turn(i):
                    after(pe, "exp_done", b * NPAIR + i + 1)
                    for t in range(KT):
                        last = tp(PS[0:KP, 3 * (i % 2) + t // 4, (t % 4) * TP:(t % 4 + 1) * TP], P[:, i % 2, t * KP:(t + 1) * KP],
                                  ident[0:TP, 0:TP])
                    last.then_inc(s["tr_ready"], 1)

                def outputs(gh, t0, t1):
                    if t0 == 0:
                        after(pe, "pt_act", b * NPAIR + 4 * gh + 4)
                        after(pe, "pt_dve", b * NPAIR + 4 * gh + 4)
                        if gh == 0:
                            after(pe, "v_act", b * 6 + 6)
                        elif prepare:
                            after(pe, "kl0_done", n * 3 + 3)
                    for t in range(t0, t1):
                        for j in range(4):
                            i = 4 * gh + j
                            last = mm(PS[32 * j:32 * j + 32, o_bank[gh], 0:TP], V[:, t, i * 32:(i + 1) * 32],
                                      PT[:, i, t * TP:(t + 1) * TP], start=t == 0, stop=t == KT - 1,
                                      tile_position=(0, 32 * j))
                    if t1 == KT:
                        last.then_inc(s["pv_ready"], 1)

                def next_context(*units):
                    if prepare:
                        for u in units:
                            context(n, u, b)

                def next_keys(*chunks):
                    if prepare:
                        for c in chunks:
                            keys(n, 0, c)

                scores(0)
                values(0)
                keys(b, 1, 0)
                scores(1)
                values(1)
                next_context(0)
                turn(0)
                keys(b, 1, 1)
                values(2)
                scores(2)
                keys(b, 1, 2)
                turn(1)
                values(3)
                next_context(1)
                scores(3)
                turn(2)
                values(4)
                scores(4)
                next_keys(0)
                next_context(2)
                turn(3)
                next_context(3)
                turn(4)
                scores(5)
                next_keys(1)
                next_context(4)
                scores(6)
                values(5)
                turn(5)
                outputs(0, 0, 3)
                scores(7)
                next_context(5)
                outputs(0, 3, 6)
                turn(6)
                next_keys(2)
                turn(7)
                outputs(0, 6, 12)
                if prepare:
                    outputs(1, 0, 12)
                else:
                    outputs(1, 0, 2)
                    pe.wait_ge(s["rden_ready"], 1)
                    after(pe, "pt_act", NPAIR * B)
                    after(pe, "pt_dve", NPAIR * B)
                    for k in range(B):
                        last = tp(PS[0:NPAIR, k // 4, (k % 4) * TP:(k % 4 + 1) * TP], den_all[:, k * NPAIR:(k + 1) * NPAIR], ident[0:TP, 0:TP])
                    last.then_inc(s["pe_post"], 1)
                    outputs(1, 2, 10)
                    pe.wait_ge(s["act_post"], 1)
                    dT_v = dT[:].rearrange("p (a k) -> p a k", a=2)
                    for t in range(TT):
                        for a in range(2):
                            last = tp(PS[0:TP, 2, t * H + a * NPAIR:t * H + (a + 1) * NPAIR], dT_v[:, a, t * TP:(t + 1) * TP], ident[0:NPAIR, 0:NPAIR])
                    last.then_inc(s["pe_post"], 1)
                    outputs(1, 10, 12)

            for u in range(5):
                context(0, u)
            pe.wait_ge(s["xq_ready"], 1)
            for h in range(NH):
                for t in range(TT):
                    last = tp(bank16(7)[:, h * T + t * TP:h * T + (t + 1) * TP], xq16[:, t, h * 128:(h + 1) * 128], ident16[0:TP, 0:TP])
            last.then_inc(s["pe_pre"], 1)
            pe.wait_ge(s["sx_diag"], 1)
            pe.wait_ge(s["dve_pre"], 1)
            for t in range(TT):
                last = mm(PS[:, 1, t * TP:(t + 1) * TP], ones[0:TP, :], diag[0:TP, t, 0:TP], start=True, stop=True)
            last.then_inc(s["pe_pre"], 1)
            context(0, 5)
            pe.wait_ge(s["wqq_ready"], 1)
            pe.wait_ge(s["act_pre"], 2)
            for h in range(NH):
                for k in range(NH):
                    last = tp(bank16(7)[:, h * D + k * 128:h * D + (k + 1) * 128], wq16[:, k, h * 128:(h + 1) * 128], ident16[:])
            last.then_inc(s["pe_pre"], 1)
            pe.wait_ge(s["act_pre"], 4)
            after(pe, "tl_done", 2)
            for k in range(NH):
                for h in range(NH):
                    last = mm(PS[:, 2 + k, 0:T], wqT[:, h, k * 128:(k + 1) * 128], xqT[:, h, :], start=h == 0, stop=h == NH - 1)
            last.then_inc(s["pe_pre"], 1)
            for c in range(CH):
                keys(0, 0, c, bank=k0_bank[c])
            for v in range(6):
                if v == 1:
                    after(pe, "kl0_done", 3)
                elif v >= 2:
                    after(pe, "v_act", v - 1)
                project_values(v, v0_bank[v])
            pe_sequence(0, True, first=True)
            with pe.Fori(1, B - 1) as b:
                pe_sequence(b, True)
            pe_sequence(B - 1, False)

            def weights_2(q, n):
                pe.wait_ge(w_in[q], n)
                for k in range(2):
                    for h in range(NH):
                        last = tp(PS[0:IH, 7, k * D + h * 128:k * D + (h + 1) * 128], w2_in[q][:, h, k * IH:(k + 1) * IH], ident[:])
                last.then_inc(s["w2t_ready"], 1)

            def weights_13(q):
                for h in range(NH):
                    for k in range(4):
                        last = tp(PS[:, 4 + h, k * IH:(k + 1) * IH], w13_in[q][:, k, h * 128:(h + 1) * 128], ident[0:IH, 0:IH])
                last.then_inc(s["w13t_ready"], 1)

            after(pe, "o_done", 2 * B)
            for t in range(TT):
                for g in range(2):
                    last = tp(PS[0:TP, out_bank[t // 2], (t % 2) * D + g * 128:(t % 2) * D + (g + 1) * 128], OT[:, g, t * TP:(t + 1) * TP], ident[:])
            last.then_inc(s["pe_post"], 1)
            pe.wait_ge(s["small_loaded"], NSMALL)
            for h in range(NH):
                last = tp(PS[:, 0, h * E:(h + 1) * E], gate_in[:, h * 128:(h + 1) * 128], ident[0:E, 0:E])
            last.then_inc(s["pe_weights"], 1)
            pe.wait_ge(s["wpq_ready"], 1)
            for h in range(NH):
                for k in range(NH):
                    tp(bank16(1)[:, h * D + k * 128:h * D + (k + 1) * 128], wp16[:, k, h * 128:(h + 1) * 128], ident16[:])
            pe.wait_ge(s["sp_diag"], 1)
            for k in range(NH):
                last = mm(PS[0:TP, 1, D + k * 128:D + (k + 1) * 128], ones[:, 0:TP], diag[:, k, :], start=True, stop=True)
            last.then_inc(s["pe_weights"], 1)
            weights_2(1, 48)
            weights_13(1)
            pe.wait_ge(s["act_weights"], 3)
            def project(k):
                pe.wait_ge(s["oqc_done"], k + 1)
                for t in range(2 * k, 2 * k + 2):
                    for h in range(NH):
                        last = mm(PS[0:TP, proj_bank[k], (t % 2) * D:(t % 2 + 1) * D], xqT[:, h, t * TP:(t + 1) * TP], wpT[:, h, :],
                                  start=h == 0, stop=h == NH - 1)
                last.then_inc(s["proj_done"], 1)

            for k in range(2):
                pe.wait_ge(s["oq_done"], k + 1)
                for h in range(NH):
                    for t in range(2):
                        last = tp(bank16(1 - k)[:, (2 * h + t) * TP:(2 * h + t + 1) * TP], xq16[:, 2 * k + t, h * 128:(h + 1) * 128],
                                  ident16[0:TP, 0:TP])
                last.then_inc(s["oqt_done"], 1)
                project(k)
            for k in range(2):
                pe.wait_ge(s["ln_done"], k + 1)
                for h in range(NH):
                    for t in range(2):
                        last = tp(PS[:, k, (2 * h + t) * TP:(2 * h + t + 1) * TP], xn[:, 2 * k + t, h * 128:(h + 1) * 128], ident[0:TP, 0:TP])
                last.then_inc(s["lnt_done"], 1)
            for k in range(2):
                pe.wait_ge(s["lnc_done"], k + 1)
                for t in range(2 * k, 2 * k + 2):
                    for h in range(NH):
                        last = mm(PS[0:TP, 3, t * E:(t + 1) * E], xT[:, h, t * TP:(t + 1) * TP], gateT[:, h, :], start=h == 0, stop=h == NH - 1)
            last.then_inc(s["pe_post"], 1)
            pe.wait_ge(s["dve_post"], 1)
            for k in range(2):
                mm(PS[0:TP, k, :], zero16[:, 0:TP], zero16[:], start=True, stop=False, skip_group_check=True)
            after(pe, "w13l_done", 1)
            for t in range(TT):
                if t == 1:
                    pe.wait_ge(s["dve_post"], 2)
                elif t == 3:
                    pe.wait_ge(s["shared_h"], 1)
                split3(PS[0:TP, g_bank[t], 0:2 * I], lambda a, h: xT16[:, a, h, t * TP:(t + 1) * TP],
                       lambda a, h: w13T[1][:, a, h, :]).then_inc(s["shared_gu"], 1)
            after(pe, "w2l_done", 1)
            after(pe, "w13l_done", 1)
            weights_2(0, 48)
            weights_13(0)
            for p in range(2):
                pe.wait_ge(s["shared_h"], 2 * p + 2)
                for k in range(2):
                    for t in range(2):
                        last = tp(PS[0:IH, h_bank[p], (k * 2 + t) * TP:(k * 2 + t + 1) * TP], hn[:, 2 * p + t, k * IH:(k + 1) * IH], ident[0:TP, 0:TP])
                last.then_inc(s["shared_ht"], 1)
            for p in range(2):
                if p == 1:
                    pe.wait_ge(s["dve_post"], 4)
                    pe.wait_ge(s["shared_h"], 3)
                    for t in range(TT):
                        for k in range(t + 1):
                            last = mm(PS[0:TP, 6, t * E:(t + 1) * E], (before16 if k == t else ones16)[:], sel16[:, k, :],
                                      start=k == 0, stop=k == t)
                    last.then_inc(s["pe_post"], 1)
                pe.wait_ge(s["shared_hl"], p + 1)
                for t in range(2):
                    for a, b in SPLIT:
                        for k in range(2):
                            last = mm(PS[0:TP, p, t * D:(t + 1) * D], hT[:, a, p, (k * 2 + t) * TP:(k * 2 + t + 1) * TP],
                                      w2T[1][:, b, k * D:(k + 1) * D], start=False, stop=False, skip_group_check=True)
                last.then_inc(s["shared_y"], 1)
            def gather(e, q):
                after(pe, "sel_done", e + 1)
                after(pe, "xg_done", e)
                for a in range(2):
                    for h in range(NH):
                        for t in range(TT):
                            last = mm(PS[:, 3, (a * NH + h) * CAP:(a * NH + h + 1) * CAP], x16[:, t, a, h * 128:(h + 1) * 128], sel[q][:, t, :],
                                      start=t == 0, stop=t == TT - 1)
                last.then_inc(s["xg_ready"], 1)

            def turn_slots(e, q):
                for t in range(TT):
                    tp(bank16(6)[:, t * TP:(t + 1) * TP], sel[q][:, t, :], ident16[0:TP, 0:TP])
                for t in range(TT):
                    last = mm(PS[:, 6, W_COL:W_COL + 2], sel[q][:, t, :], wt16[:].rearrange("p t e k -> p t (e k)")[:, t, bass.ds(e * 2, 2)],
                              start=t == 0, stop=t == TT - 1)
                last.then_inc(s["st_ready"], 1)

            def add(e, q, final=False):
                for t in range(TT):
                    for a in range(2):
                        last = mm(PS[0:TP, t // 2, (t % 2) * D:(t % 2 + 1) * D], selT[q][:, t * TP:(t + 1) * TP], y16[:, a, :],
                                  start=False, stop=final and a == 1, skip_group_check=True)
                last.then_inc(s["added"], 1)

            def expert(e, q, prepare):
                if prepare is not None:
                    after(pe, "w2l_done", e + 2)
                    weights_2(1 - q, prepare)
                after(pe, "w13l_done", e + 2)
                after(pe, "xg_done", e + 1)
                after(pe, "st_done", e + 1)
                after(pe, "slot_w_done", e + 1)
                split3(PS[:, 6, 0:2 * I], lambda a, h: xeT[:, a, h, :], lambda a, h: w13T[q][:, a, h, :]).then_inc(s["gu_ready"], 1)
                if prepare is not None:
                    weights_13(1 - q)
                    gather(e + 1, 1 - q)
                after(pe, "h_done", e + 1)
                after(pe, "yl_done", e)
                for k in range(2):
                    last = tp(PS[0:IH, 2, k * CAP:(k + 1) * CAP], hn_e[:, k * IH:(k + 1) * IH], ident[:])
                last.then_inc(s["ht_ready"], 1)
                if prepare is not None:
                    turn_slots(e + 1, 1 - q)
                add(e - 1, 1 - q)
                after(pe, "hl_done", e + 1)
                after(pe, "w2l_done", e + 2)
                split3(PS[:, 2, 0:D], lambda a, k: heT[:, a, k * CAP:(k + 1) * CAP], lambda a, k: w2T[q][:, a, k * D:(k + 1) * D]).then_inc(s["y_ready"], 1)

            pe.wait_ge(s["x16_ready"], 1)
            pe.wait_ge(s["dve_post"], 5)
            gather(0, 0)
            turn_slots(0, 0)
            pe.wait_ge(s["added_init"], 2)
            with pe.Fori(0, E // 2 - 1) as it:
                expert(it * 2, 0, it * 48 + 96)
                expert(it * 2 + 1, 1, it * 48 + 96)
            expert(E - 2, 0, (E // 2 + 1) * 48)
            expert(E - 1, 1, None)
            after(pe, "yl_done", E)
            add(E - 1, 1, final=True)


_INS = ["x", "ctx_2048", "g_xattn", "g_ffn", "L0_xattn_wq", "L0_xattn_bq", "L0_xattn_wkv", "L0_xattn_bkv",
        "L0_xattn_wp", "L0_xattn_bp", "L0_ffn_gate_w", "L0_ffn_gate_b", "L0_ffn_W1", "L0_ffn_W3", "L0_ffn_W2",
        "L0_ffn_Ws1", "L0_ffn_Ws3", "L0_ffn_Ws2"]


def kernel(**inputs):
    import numpy as np
    import concourse.bacc as bacc
    from concourse.bass_utils import run_bass_kernel_spmd

    nc = bacc.Bacc("TRN2", target_bir_lowering=False, num_devices=1)
    arrays, args = {}, []
    for name in _INS:
        a = np.ascontiguousarray(inputs[name])
        arrays[name] = a
        args.append(nc.dram_tensor(name, a.shape, mybir.dt.from_np(a.dtype), kind="ExternalInput").ap())
    args.append(nc.dram_tensor("y", (B, S, D), F32, kind="ExternalOutput").ap())
    program(nc, *args)
    return run_bass_kernel_spmd(nc, [arrays], core_ids=[0]).results[0]["y"]
```
